# Optimizing a Trainium2 kernel written in Bass

```python
import numpy as np
import jax
import jax.numpy as jnp

def _softmax(x, axis=-1):
    return jax.nn.softmax(x, axis=axis)

def _gelu(x):
    return jax.nn.gelu(x, approximate=True)

def _silu(x):
    return jax.nn.silu(x)

def _sigmoid(x):
    return jax.nn.sigmoid(x)

def _layernorm(x, axis=-1, eps=1e-05):
    m = jnp.mean(x, axis=axis, keepdims=True)
    v = jnp.var(x, axis=axis, keepdims=True)
    return (x - m) / jnp.sqrt(v + eps)

def _scatter_add(tgt, idx, src, axis=0):
    return tgt.at[idx].add(src)

def _segment_sum(src, seg, n):
    return jax.ops.segment_sum(src, seg, n)
kernel_name = 'mk_macaron_d1_jaxref_r8_93d57e'

def setup_inputs(seed: int=0):
    np.random.seed(seed)
    _w = jnp.asarray

    def _L0_attn_setup():
        import jax, jax.numpy as jnp
        import numpy as np
        B, L, IN_DIM = (4, 256, 128)
        H, D = (16, 64)
        OUT_DIM = 128
        key = jax.random.key(seed)
        k1, k2, k3 = jax.random.split(key, 3)
        inputs = jax.random.normal(k1, (B, L, IN_DIM), dtype=jnp.float32)
        W_qkv = jax.random.normal(k2, (IN_DIM, 3 * H * D), dtype=jnp.float32) * IN_DIM ** (-0.5)
        W_out = jax.random.normal(k3, (H * D, OUT_DIM), dtype=jnp.float32) * (H * D) ** (-0.5)
        return {'inputs': inputs, 'W_qkv': W_qkv, 'W_out': W_out}
    _L0_attn_in = _L0_attn_setup()

    def _L0_ffn_setup():
        import jax, jax.numpy as jnp
        import numpy as np
        E, K = (8, 4)
        B, S, D = (4, 128, 128)
        H = D * 2 * 4 // 3

        def _swiglu(u, w1, w2, w3):
            h = jnp.einsum('...d,hd->...h', u, w1)
            v = jnp.einsum('...d,hd->...h', u, w2)
            return jnp.einsum('...h,dh->...d', jax.nn.sigmoid(h) * h * v, w3)
        key = jax.random.key(seed)
        ks = jax.random.split(key, 9)
        std = 0.02
        return {'x': jax.random.normal(ks[0], (B, S, D), jnp.float32), 'Wg': jax.random.normal(ks[1], (E, D), jnp.float32) * std, 'routing_bias': jnp.zeros((E,), jnp.float32), 'W1': jax.random.normal(ks[2], (E, H, D), jnp.float32) * std, 'W2': jax.random.normal(ks[3], (E, H, D), jnp.float32) * std, 'W3': jax.random.normal(ks[4], (E, D, H), jnp.float32) * std, 'Ws1': jax.random.normal(ks[5], (H, D), jnp.float32) * std, 'Ws2': jax.random.normal(ks[6], (H, D), jnp.float32) * std, 'Ws3': jax.random.normal(ks[7], (D, H), jnp.float32) * std}
    _L0_ffn_in = _L0_ffn_setup()
    _d = {'L0_attn_inputs': _L0_attn_in['inputs'], 'L0_attn_W_qkv': _L0_attn_in['W_qkv'], 'L0_attn_W_out': _L0_attn_in['W_out'], 'L0_ffn_Wg': _L0_ffn_in['Wg'], 'L0_ffn_routing_bias': _L0_ffn_in['routing_bias'], 'L0_ffn_W1': _L0_ffn_in['W1'], 'L0_ffn_W2': _L0_ffn_in['W2'], 'L0_ffn_W3': _L0_ffn_in['W3'], 'L0_ffn_Ws1': _L0_ffn_in['Ws1'], 'L0_ffn_Ws2': _L0_ffn_in['Ws2'], 'L0_ffn_Ws3': _L0_ffn_in['Ws3']}
    _x0 = _d['L0_attn_inputs']
    _d['L0_attn_inputs'] = jax.random.normal(jax.random.fold_in(jax.random.key(seed), 1), (4, 512, 128), dtype=_x0.dtype)
    del _x0
    return _d

def reference(L0_attn_inputs, L0_attn_W_qkv, L0_attn_W_out, L0_ffn_Wg, L0_ffn_routing_bias, L0_ffn_W1, L0_ffn_W2, L0_ffn_W3, L0_ffn_Ws1, L0_ffn_Ws2, L0_ffn_Ws3):

    def _L0_attn_ref(inputs, W_qkv, W_out):
        import jax, jax.numpy as jnp
        import numpy as np
        B, L, IN_DIM = (4, 256, 128)
        H, D = (16, 64)
        OUT_DIM = 128
        b, l, _ = inputs.shape
        qkv = inputs @ W_qkv
        q, k, v = jnp.split(qkv, 3, axis=-1)
        q = q.reshape(b, l, H, D)
        k = k.reshape(b, l, H, D)
        v = v.reshape(b, l, H, D)
        score = jnp.einsum('bihd,bjhd->bijh', q, k) / D ** 0.5
        mask = jnp.tril(jnp.ones((l, l), dtype=score.dtype))[None, :, :, None]
        masked_score = score * mask + 1e+30 * (mask - 1.0)
        wmat = jax.nn.softmax(masked_score, axis=2)
        out = jnp.einsum('bijh,bjhd->bihd', wmat, v).reshape(b, l, H * D)
        return out @ W_out

    def _L0_ffn_ref(x, Wg, routing_bias, W1, W2, W3, Ws1, Ws2, Ws3):
        import jax, jax.numpy as jnp
        import numpy as np
        E, K = (8, 4)
        B, S, D = (4, 128, 128)
        H = D * 2 * 4 // 3

        def _swiglu(u, w1, w2, w3):
            h = jnp.einsum('...d,hd->...h', u, w1)
            v = jnp.einsum('...d,hd->...h', u, w2)
            return jnp.einsum('...h,dh->...d', jax.nn.sigmoid(h) * h * v, w3)
        gate = jnp.einsum('bsd,ed->bse', x, Wg) + routing_bias
        _, top_idx = jax.lax.top_k(gate, K)
        mask = jax.nn.one_hot(top_idx, E, dtype=gate.dtype).sum(-2)
        masked_gate = jnp.where(mask > 0, gate, -jnp.inf)
        probs = jax.nn.softmax(masked_gate, axis=-1)
        weights = probs * mask
        out = _swiglu(x, Ws1, Ws2, Ws3)
        h1 = jnp.einsum('bsd,ehd->ebsh', x, W1)
        h2 = jnp.einsum('bsd,ehd->ebsh', x, W2)
        eo = jnp.einsum('ebsh,edh->ebsd', jax.nn.sigmoid(h1) * h1 * h2, W3)
        out = out + jnp.einsum('ebsd,bse->bsd', eo, weights)
        return out
    x = L0_attn_inputs
    x = x + 0.5 * _L0_ffn_ref(_layernorm(x, axis=-1), L0_ffn_Wg, L0_ffn_routing_bias, L0_ffn_W1, L0_ffn_W2, L0_ffn_W3, L0_ffn_Ws1, L0_ffn_Ws2, L0_ffn_Ws3)
    x = x + _L0_attn_ref(_layernorm(x, axis=-1), L0_attn_W_qkv, L0_attn_W_out)
    x = x + 0.5 * _L0_ffn_ref(_layernorm(x, axis=-1), L0_ffn_Wg, L0_ffn_routing_bias, L0_ffn_W1, L0_ffn_W2, L0_ffn_W3, L0_ffn_Ws1, L0_ffn_Ws2, L0_ffn_Ws3)
    return x

_drawn_inputs = setup_inputs


def setup_inputs(seed=0):
    import zlib

    import numpy as np

    out = dict(_drawn_inputs(seed))
    spreads = {'L0_ffn_routing_bias': (0.0, 0.8)}
    factors = {'L0_ffn_Wg': 8.0,
     'L0_ffn_W1': 8.0,
     'L0_ffn_W2': 8.0,
     'L0_ffn_W3': 8.0,
     'L0_ffn_Ws1': 6.105,
     'L0_ffn_Ws2': 6.013,
     'L0_ffn_Ws3': 6.045}
    for name, (base, spread) in spreads.items():
        noise = np.random.default_rng([zlib.crc32(name.encode()), seed]).standard_normal(out[name].shape)
        drawn = base * np.exp(spread * noise) if base else spread * noise
        out[name] = jnp.asarray(drawn.astype(out[name].dtype))
    for name, factor in factors.items():
        out[name] = (out[name] * factor).astype(out[name].dtype)
    return out
```

```python
from contextlib import ExitStack

import concourse.bass as bass
from concourse import mybir

F32 = mybir.dt.float32
F32R = mybir.dt.float32r
F16 = mybir.dt.float16
BF16 = mybir.dt.bfloat16
U32 = mybir.dt.uint32
ALU = mybir.AluOpType
ACT = mybir.ActivationFunctionType
AX = mybir.AxisListType

P = 128
LN_EPS = 1e-5
TOP_K = 4
MASKED = -8e30
P_SCALE = 4096.0


class Signal:

    def __init__(self, sem):
        self.sem, self.value = sem, 0


class Queue:

    def __init__(self):
        self.steps, self.passed = [], {}

    def wait(self, *tokens):
        for signal, value in tokens:
            if self.passed.get(signal, 0) < value:
                self.passed[signal] = value
                self.steps.append(lambda eng, s=signal.sem, v=value: eng.wait_ge(s, v))

    def do(self, issue, signal=None, by=1):
        if signal is None:
            self.steps.append(issue)
            return None
        self.steps.append(lambda eng: issue(eng).then_inc(signal.sem, by))
        signal.value += by
        return signal, signal.value

    def play(self, eng):
        for step in self.steps:
            step(eng)


class Buffer:

    def __init__(self, tensor):
        self.t, self.free, self.ready = tensor, [], []


class Ring:
    def __init__(self, buffers):
        self.buffers, self.taken = buffers, 0

    def take(self):
        self.taken += 1
        return self.buffers[(self.taken - 1) % len(self.buffers)]


def macaron(nc, x, w_qkv, w_out, w_gate, routing_bias, w1, w2, w3, ws1, ws2, ws3, out, weight_scratch):
    B, L, D = x.shape
    E, HID, _ = w1.shape
    NE = E + 1
    NT = L // P
    INNER = w_out.shape[0]
    HEAD = 64
    PAIRS = INNER // P
    TILES = [(j * P, min(P, HID - j * P)) for j in range((HID + P - 1) // P)]
    NJ = len(TILES)
    assert D == P and L == 512 and NJ == 3 and 2 * HEAD == P

    with ExitStack() as ctx:
        def sb(name, shape, dt=F32):
            return ctx.enter_context(nc.sbuf_tensor(name, shape, dt))

        def bank(name):
            return Buffer(ctx.enter_context(nc.psum_tensor(name, [P, 512], F32)))

        def signal(name):
            return Signal(ctx.enter_context(nc.semaphore(name)))

        w1h, w1l = sb("w1h", [P, NE, HID], F32R), sb("w1l", [P, NE, HID], F32R)
        w2h, w2l = sb("w2h", [P, NE, HID], F32R), sb("w2l", [P, NE, HID], F32R)
        w3h, w3l = sb("w3h", [P, NE, NJ, D], F32R), sb("w3l", [P, NE, NJ, D], F32R)
        wqkvh, wqkvl = sb("wqkvh", [P, 3 * INNER], F32R), sb("wqkvl", [P, 3 * INNER], F32R)
        woh, wol = sb("woh", [P, PAIRS, D], F32R), sb("wol", [P, PAIRS, D], F32R)
        wgh, wgl = sb("wgh", [P, E], F32R), sb("wgl", [P, E], F32R)

        ident = sb("ident", [P, P])
        ident_b = sb("ident_b", [P, P], BF16)
        causal = sb("causal", [P, P], BF16)
        earlier = sb("earlier", [P, E, E])
        neg_half = sb("neg_half", [P, NT])
        bias_b = sb("bias_b", [P, E])
        v_max = sb("v_max", [P, 1])
        v_top = sb("v_top", [P, 1])
        v_pow = sb("v_pow", [P, 1])
        v_inv = sb("v_inv", [P, 1])
        v_scale = sb("v_scale", [P, 1])
        pv_scale = sb("pv_scale", [P, 1])

        xs = sb("xs", [P, B * NT, D])
        xs_ready = [[] for _ in range(B)]
        xn = Buffer(sb("xn", [P, NT, D]))
        stats = sb("stats", [P, NT, 6])
        moments = sb("moments", [P, NT, 2])
        var_eps = sb("var_eps", [P, NT])
        rstd = sb("rstd", [P, NT])
        xnT = Ring([(Buffer(sb(f"xnTh{i}", [P, L], F32R)), Buffer(sb(f"xnTl{i}", [P, L], F32R))) for i in range(2)])

        gate = sb("gate", [P, NT, E])
        top = sb("top", [P, NT])
        beats, ties = [xn.t[:, :, :].rearrange("p t d -> p (t d)")[:, k * NT * E * E:(k + 1) * NT * E * E]
                       .rearrange("p (t i j) -> p t i j", t=NT, i=E) for k in range(2)]
        rank = sb("rank", [P, NT, E])
        shifted = sb("shifted", [P, NT, E])
        expo = sb("expo", [P, NT, E])
        chosen = sb("chosen", [P, NT, E])
        total = sb("total", [P, NT])
        inv_total = sb("inv_total", [P, NT])
        route = Buffer(sb("route", [P, NT, E]))
        routeT = Buffer(sb("routeT", [NT * E, P]))
        wide = Ring([Buffer(sb(f"wide{i}", [P, NT, P])) for i in range(2)])

        silu = Ring([Buffer(sb(f"silu{i}", [P, L])) for i in range(2)])
        glu = Ring([Buffer(sb(f"glu{i}", [P, L])) for i in range(2)])
        gluh = Ring([Buffer(sb(f"gluh{i}", [P, L], F32R)) for i in range(3)])
        glul = Ring([Buffer(sb(f"glul{i}", [P, L], F32R)) for i in range(3)])
        acc = Buffer(sb("acc", [P, L]))
        part = Buffer(sb("part", [P, L]))

        qk = [[Buffer(sb(f"{n}{i}", [P, L], F32R)) for n in ("qh", "ql", "kh", "kl")] for i in range(2)]
        vh, vl = Buffer(sb("vh", [P, NT, INNER], F16)), Buffer(sb("vl", [P, NT, INNER], F16))
        probs = Ring([Buffer(sb(f"probs{i}", [P, 512])) for i in range(3)])
        pTh = Ring([Buffer(sb(f"pTh{i}", [P, 512], F16)) for i in range(3)])
        pTl = Ring([Buffer(sb(f"pTl{i}", [P, 512], F16)) for i in range(3)])
        neg_max = sb("neg_max", [P, 2, NT, 2])
        row_sum = sb("row_sum", [P, 2, NT, 2])
        scaled_sum = sb("scaled_sum", [P, 2, NT, 2])
        inv_sum = sb("inv_sum", [P, 2, NT, 2])
        attn = Buffer(sb("attn", [P, NT, P]))
        aTh, aTl = Buffer(sb("aTh", [P, L], F32R)), Buffer(sb("aTl", [P, L], F32R))
        raw12 = [vh.t[:, :, :].rearrange("p t n -> p (t n)")[:, i * 1536:(i + 1) * 1536].bitcast(F32)
                 .rearrange("p (w j d) -> p w j d", w=2, j=3) for i in range(2)]
        raw3 = [vl.t[:, :, :].rearrange("p t n -> p (t n)")[:, i * 1024:i * 1024 + 2 * HID].bitcast(F32)
                for i in range(2)]
        raw_w = [probs.buffers[i].t[:, :] for i in range(2)]

        banks = Ring([bank(f"bank{i}") for i in range(4)])
        down_bank, y_bank = bank("down_bank"), bank("y_bank")
        o_banks = [bank("o_bank0"), bank("o_bank1")]

        x_in = [signal(f"x_in{b}") for b in range(B)]
        small_in = signal("small_in")
        raw_in = [signal(f"raw_in{i}") for i in range(2)]
        raw_w_in = [signal(f"raw_w_in{i}") for i in range(2)]
        route_stored = signal("route_stored")
        wide_in = [signal(f"wide_in{i}") for i in range(2)]
        stored = signal("stored")
        consts_made = signal("consts_made")
        pool_split = signal("pool_split")
        pool_small = signal("pool_small")
        turned = signal("turned")
        hidden_done = signal("hidden_done")
        down_done = signal("down_done")
        gate_done = signal("gate_done")
        qk_done = signal("qk_done")
        v_done = signal("v_done")
        scores_done = signal("scores_done")
        pv_done = signal("pv_done")
        y_done = signal("y_done")
        act_high = signal("act_high")
        act_silu = signal("act_silu")
        act_exp = signal("act_exp")
        act_copy = signal("act_copy")
        dve_low = signal("dve_low")
        dve_glu = signal("dve_glu")
        dve_acc = signal("dve_acc")
        dve_small = signal("dve_small")
        dve_max = signal("dve_max")

        SP, POOL, PE, ACTQ, DVE = Queue(), Queue(), Queue(), Queue(), Queue()

        def f32(ap):
            return ap.bitcast(F32)

        chunk_of = lambda t, b: t[b].rearrange("(t p) d -> p t d", p=P)
        x_tok = [SP.do(lambda e, b=b: e.dma_start(xs[:, b * NT:(b + 1) * NT, :], chunk_of(x, b)), x_in[b], 16)
                 for b in range(1)]
        wg_raw = attn.t[0:E, 0, :]
        SP.do(lambda e: e.dma_start(wg_raw, w_gate), small_in, 16)
        small_tok = SP.do(lambda e: e.dma_start(bias_b[:, :], routing_bias.rearrange("(a n) -> a n", a=1)
                                                .broadcast_to([P, E])), small_in, 16)

        raw_free = [[], []]
        raw_ready = {}

        def load_expert(n):
            i = n % 2
            SP.wait(*raw_free[i])
            srcs = [ws1, ws2] if n == 0 else [w1[n - 1], w2[n - 1]]
            for k, src in enumerate(srcs):
                SP.do(lambda e, k=k, src=src: e.dma_start(
                    raw12[i][:, k, 0:2, :], src[0:2 * P, :].rearrange("(j p) d -> p j d", p=P)), raw_in[i], 16)
                SP.do(lambda e, k=k, src=src: e.dma_start(raw12[i][0:HID - 2 * P, k, 2, :], src[2 * P:HID, :]),
                      raw_in[i], 16)
            raw_ready[n] = SP.do(lambda e: e.dma_start(raw3[i], ws3 if n == 0 else w3[n - 1]), raw_in[i], 16)

        raw_w_free = [[], []]
        wide_weights = [(w_qkv[:, c * 512:(c + 1) * 512], wqkvh[:, c * 512:(c + 1) * 512],
                         wqkvl[:, c * 512:(c + 1) * 512]) for c in range(3 * INNER // 512)]
        wide_weights += [(w_out.rearrange("(k p) d -> p k d", p=P)[:, 4 * c:4 * c + 4, :],
                          woh[:, 4 * c:4 * c + 4, :], wol[:, 4 * c:4 * c + 4, :]) for c in range(PAIRS // 4)]
        attn_weights = []

        def load_attention_weight(c):
            src, high, low = wide_weights[c]
            i = c % 2
            raw = raw_w[i] if c < 3 * INNER // 512 else raw_w[i].rearrange("p (k d) -> p k d", k=4)
            SP.wait(*raw_w_free[i])
            tok = SP.do(lambda e: e.dma_start(raw, src), raw_w_in[i], 16)
            POOL.wait(tok)
            tok = POOL.do(lambda e: e.tensor_copy(high, raw), pool_split)
            POOL.wait(tok)
            tok = POOL.do(lambda e: e.tensor_tensor(low, raw, f32(high), ALU.subtract), pool_split)
            raw_w_free[i] = [tok]
            attn_weights.append(tok)

        POOL.do(lambda e: e.memset(ident[:, :], 0.0), consts_made)
        POOL.do(lambda e: e.memset(causal[:, :], 0.0), consts_made)
        POOL.do(lambda e: e.memset(earlier[:, :, :], 1.0), consts_made)
        tok = POOL.do(lambda e: e.memset(neg_half[:, :], -0.5), consts_made)
        POOL.wait(tok)
        tok = POOL.do(lambda e: e.affine_select(out=ident[:, :], in_=ident[:, :], compare_op=ALU.not_equal, fill=1.0,
                                                base=0, pattern=[[-1, P]], channel_multiplier=1), consts_made)
        POOL.do(lambda e: e.affine_select(out=causal[:, :], in_=causal[:, :], compare_op=ALU.is_ge, fill=MASKED,
                                          base=0, pattern=[[-1, P]], channel_multiplier=1), consts_made)
        POOL.do(lambda e: e.affine_select(out=earlier[:, :, :], in_=earlier[:, :, :], compare_op=ALU.is_gt, fill=0.0,
                                          base=0, pattern=[[1, E], [-1, E]], channel_multiplier=0), consts_made)
        POOL.wait(tok)
        consts = POOL.do(lambda e: e.tensor_copy(ident_b[:, :], ident[:, :]), consts_made)

        bk = banks.take()
        PE.wait(consts, small_tok)
        tok = PE.do(lambda e: e.transpose(bk.t[:, 0:E], wg_raw, ident[0:E, 0:E]), turned)
        attn.free = [tok]
        ACTQ.wait(tok)
        tok = ACTQ.do(lambda e: e.activation(wgh[:, :], bk.t[:, 0:E], ACT.Copy), act_high)
        DVE.wait(tok)
        gate_weights = DVE.do(lambda e: e.tensor_tensor(wgl[:, :], bk.t[:, 0:E], f32(wgh[:, :]), ALU.subtract), dve_low)
        bk.free = [gate_weights]

        def split_bank(src, high, low, after, scale=None):
            ACTQ.wait(*after)
            t_high = ACTQ.do(lambda e: e.activation(high, src, ACT.Copy, scale=1.0 if scale is None else scale),
                             act_high)
            DVE.wait(t_high)
            hv = f32(high) if high.dtype == F32R else high
            if scale is None:
                t_low = DVE.do(lambda e: e.tensor_tensor(low, src, hv, ALU.subtract), dve_low)
            else:
                t_low = DVE.do(lambda e: e.scalar_tensor_tensor(low, src, scale, hv, ALU.mult, ALU.subtract), dve_low)
            return [t_high, t_low]

        expert_ready = {}

        def prepare_expert(n):
            i = n % 2
            PE.wait(raw_ready[n])
            ready = []
            for k, (high, low) in enumerate(((w1h, w1l), (w2h, w2l))):
                bk = banks.take()
                PE.wait(*bk.free)
                for j, (h0, m) in enumerate(TILES):
                    last = j == NJ - 1
                    tok = PE.do(lambda e, j=j, h0=h0, m=m, k=k, bk=bk: e.transpose(
                        bk.t[:, h0:h0 + m], raw12[i][0:m, k, j, :], ident[0:m, 0:m]), turned if last else None)
                bk.free = split_bank(bk.t[:, 0:HID], high[:, n, :], low[:, n, :], [tok])
                ready += bk.free
            bk = banks.take()
            PE.wait(*bk.free)
            for j, (h0, m) in enumerate(TILES):
                tok = PE.do(lambda e, j=j, h0=h0, m=m, bk=bk: e.transpose(
                    bk.t[0:m, j * D:(j + 1) * D], raw3[i][:, h0:h0 + m], ident[:, :]),
                    turned if j == NJ - 1 else None)
            raw_free[i] = [tok]
            m = TILES[-1][1]
            both = split_bank(bk.t[:, 0:2 * D], w3h[:, n, 0:2, :].rearrange("p j d -> p (j d)"),
                              w3l[:, n, 0:2, :].rearrange("p j d -> p (j d)"), [tok])
            DVE.wait(both[0])
            tail = split_bank(bk.t[0:m, 2 * D:3 * D], w3h[0:m, n, 2, :], w3l[0:m, n, 2, :], [tok, both[1]])
            bk.free = tail
            expert_ready[n] = ready + both + tail

        def three_pass(ps, high, low, mhigh, mlow, signal=None, first=True, last=True):
            PE.do(lambda e: e.matmul(ps, high, mhigh, start=first, stop=False))
            PE.do(lambda e: e.matmul(ps, high, mlow, start=False, stop=False))
            return PE.do(lambda e: e.matmul(ps, low, mhigh, start=False, stop=last), signal)

        def layer_norm(b):
            rows = [xs[:, b * NT + t, :] for t in range(NT)]
            DVE.wait(*xs_ready[b])
            for t in range(NT):
                tok = DVE.do(lambda e, t=t: e.bn_stats(stats[:, t, :], rows[t]), dve_small)
            DVE.wait(tok)
            for t in range(NT):
                tok = DVE.do(lambda e, t=t: e.bn_aggr(moments[:, t, :], stats[:, t, :]), dve_small)
            DVE.wait(tok)
            tok = DVE.do(lambda e: e.tensor_scalar(var_eps[:, :], moments[:, :, 1], LN_EPS, None, ALU.add), dve_small)
            POOL.wait(tok, consts)
            tok = POOL.do(lambda e: e.tensor_tensor(rstd[:, :], var_eps[:, :], neg_half[:, :], ALU.pow), pool_small)
            DVE.wait(tok, *xn.free)
            for t in range(NT):
                tok = DVE.do(lambda e, t=t: e.tensor_scalar(xn.t[:, t, :], rows[t], moments[:, t, 0:1],
                                                            rstd[:, t:t + 1], ALU.subtract, ALU.mult), dve_small)
            bk = banks.take()
            PE.wait(tok, *bk.free)
            for t in range(NT):
                tok = PE.do(lambda e, t=t: e.transpose(bk.t[:, t * P:(t + 1) * P], xn.t[:, t, :], ident[:, :]),
                            turned if t == NT - 1 else None)
            xn.free = [tok]
            xh, xl = xnT.take()
            ACTQ.wait(*xh.free)
            DVE.wait(*xl.free)
            bk.free = split_bank(bk.t[:, :], xh.t[:, :], xl.t[:, :], [tok])
            xh.ready = xl.ready = bk.free
            return xh, xl

        scratch_ready = {}

        def router(c, b, xh, xl):
            bk = banks.take()
            PE.wait(*bk.free, *xh.ready, gate_weights)
            for t in range(NT):
                s = slice(t * P, (t + 1) * P)
                tok = three_pass(bk.t[:, t * E:(t + 1) * E], xh.t[:, s], xl.t[:, s], wgh[:, :], wgl[:, :],
                                 gate_done if t == NT - 1 else None)
            rows_i = lambda a: a[:, :, :].unsqueeze(3).broadcast_to([P, NT, E, E])
            rows_j = lambda a: a[:, :, :].unsqueeze(2).broadcast_to([P, NT, E, E])
            over = lambda a: a[:, :].unsqueeze(2).broadcast_to([P, NT, E])

            def small(issue, *waits):
                DVE.wait(*waits)
                return DVE.do(issue, dve_small)

            tok = small(lambda e: e.tensor_tensor(gate[:, :, :], bk.t[:, 0:NT * E].rearrange("p (t n) -> p t n", t=NT),
                                                  bias_b[:, :].unsqueeze(1).broadcast_to([P, NT, E]), ALU.add),
                        tok, small_tok)
            bk.free = [tok]
            t_top = small(lambda e: e.tensor_reduce(top[:, :], gate[:, :, :], AX.X, ALU.max), tok)
            small(lambda e: e.tensor_tensor(beats, rows_j(gate), rows_i(gate), ALU.is_gt))
            tok = small(lambda e: e.tensor_tensor(ties, rows_j(gate), rows_i(gate), ALU.is_equal))
            t_shift = small(lambda e: e.tensor_tensor(shifted[:, :, :], gate[:, :, :], over(top), ALU.subtract), t_top)
            tok = small(lambda e: e.tensor_tensor(ties, ties,
                                                  earlier[:, :, :].unsqueeze(1).broadcast_to([P, NT, E, E]), ALU.mult),
                        tok, consts)
            ACTQ.wait(t_shift)
            t_exp = ACTQ.do(lambda e: e.activation(expo[:, :, :], shifted[:, :, :], ACT.Exp), act_exp)
            tok = small(lambda e: e.tensor_tensor(beats, beats, ties, ALU.add), tok)
            tok = small(lambda e: e.tensor_reduce(rank[:, :, :], beats, AX.X, ALU.add), tok)
            tok = small(lambda e: e.scalar_tensor_tensor(chosen[:, :, :], rank[:, :, :], float(TOP_K), expo[:, :, :],
                                                         ALU.is_lt, ALU.mult), tok, t_exp)
            tok = small(lambda e: e.tensor_reduce(total[:, :], chosen[:, :, :], AX.X, ALU.add), tok)
            tok = small(lambda e: e.reciprocal(inv_total[:, :], total[:, :]), tok)
            tok = small(lambda e: e.scalar_tensor_tensor(route.t[:, :, :], chosen[:, :, :], 0.5, over(inv_total),
                                                         ALU.mult, ALU.mult), tok, *route.free)
            bt = banks.take()
            PE.wait(tok, *bt.free)
            tok = PE.do(lambda e: e.transpose(bt.t[0:NT * E, 0:P], route.t[:, :, :].rearrange("p t n -> p (t n)"),
                                              ident[:, :]), turned)
            route.free = [tok]
            DVE.wait(tok, *routeT.free)
            tok = DVE.do(lambda e: e.tensor_copy(routeT.t[:, :], bt.t[0:NT * E, 0:P]), dve_small)
            bt.free = [tok]
            SP.wait(tok)
            tok = SP.do(lambda e: e.dma_start(weight_scratch[c], routeT.t[:, :]), route_stored, 16)
            routeT.free = [tok]
            scratch_ready[c] = tok

        def widen(c, e_n):
            n = wide.taken % 2
            buf = wide.take()
            SP.wait(scratch_ready[c], *buf.free)
            src = weight_scratch[c].rearrange("(t n) p -> n t p", t=NT)[e_n:e_n + 1].broadcast_to([P, NT, P])
            buf.ready = [SP.do(lambda e: e.dma_start(buf.t[:, :, :], src), wide_in[n], 16)]
            return buf

        def feed_forward(c, b, xh, xl, prepare):
            work = [(n, j) for n in range(NE) for j in range(NJ)]
            tiles = {}
            if prepare:
                load_expert(0)
                load_expert(1)
                prepare_expert(0)
                router(c, b, xh, xl)

            def hidden(i):
                n, j = work[i]
                h0, m = TILES[j]
                b1, b2 = banks.take(), banks.take()
                PE.wait(*b1.free, *xh.ready, *expert_ready[n])
                t1 = three_pass(b1.t[0:m, :], w1h[:, n, h0:h0 + m], w1l[:, n, h0:h0 + m], xh.t[:, :], xl.t[:, :],
                                hidden_done)
                PE.wait(*b2.free)
                t2 = three_pass(b2.t[0:m, :], w2h[:, n, h0:h0 + m], w2l[:, n, h0:h0 + m], xh.t[:, :], xl.t[:, :],
                                hidden_done)
                s, g, gh, gl = silu.take(), glu.take(), gluh.take(), glul.take()
                ACTQ.wait(t1, *s.free)
                ts = ACTQ.do(lambda e: e.activation(s.t[0:m, :], b1.t[0:m, :], ACT.Silu), act_silu)
                b1.free = [ts]
                DVE.wait(t2, ts, *g.free)
                tg = DVE.do(lambda e: e.tensor_tensor(g.t[0:m, :], s.t[0:m, :], b2.t[0:m, :], ALU.mult), dve_glu)
                b2.free = s.free = [tg]
                ACTQ.wait(tg, *gh.free)
                th = ACTQ.do(lambda e: e.activation(gh.t[0:m, :], g.t[0:m, :], ACT.Copy), act_high)
                POOL.wait(th, tg, *gl.free)
                tl = POOL.do(lambda e: e.tensor_tensor(gl.t[0:m, :], g.t[0:m, :], f32(gh.t[0:m, :]), ALU.subtract),
                             pool_split)
                g.free = [th, tl]
                tiles[i] = (gh, gl, [th, tl])

            def down(i):
                n, j = work[i]
                m = TILES[j][1]
                gh, gl, ready = tiles.pop(i)
                PE.wait(*ready)
                if j == 0:
                    PE.wait(*down_bank.free)
                tok = three_pass(down_bank.t[:, :], w3h[0:m, n, j, :], w3l[0:m, n, j, :], gh.t[0:m, :], gl.t[0:m, :],
                                 down_done, first=j == 0, last=j == NJ - 1)
                gh.free = gl.free = [tok]
                if j < NJ - 1:
                    return
                if n == 0:
                    DVE.wait(tok, *acc.free)
                    tok = DVE.do(lambda e: e.tensor_scalar(acc.t[:, :], down_bank.t[:, :], 0.5, None, ALU.mult),
                                 dve_acc)
                    down_bank.free = acc.ready = [tok]
                    return
                w = wides.pop(n)
                DVE.wait(tok, *w.ready, *part.free)
                tok = DVE.do(lambda e: e.tensor_tensor(part.t[:, :], down_bank.t[:, :],
                                                       w.t[:, :, :].rearrange("p t n -> p (t n)"), ALU.mult), dve_acc)
                w.free = down_bank.free = [tok]
                DVE.wait(tok, *acc.ready)
                tok = DVE.do(lambda e: e.tensor_tensor(acc.t[:, :], acc.t[:, :], part.t[:, :], ALU.add), dve_acc)
                part.free = acc.ready = [tok]

            wides = {}
            LAG = 2
            for i in range(len(work) + LAG):
                if i < len(work):
                    n, j = work[i]
                    if j == 0 and n + 1 < NE and prepare:
                        prepare_expert(n + 1)
                        if n + 2 < NE:
                            load_expert(n + 2)
                    hidden(i)
                if i >= LAG:
                    down(i - LAG)
                if i < len(work) and j == NJ - 1 and n + 1 < NE:
                    wides[n + 1] = widen(c, n)
                yield
            xh.free = xl.free = [(hidden_done, hidden_done.value)]
            bk = banks.take()
            PE.wait(*acc.ready, *bk.free)
            for t in range(NT):
                tok = PE.do(lambda e, t=t: e.transpose(bk.t[:, t * P:(t + 1) * P], acc.t[:, t * P:(t + 1) * P],
                                                       ident[:, :]), turned if t == NT - 1 else None)
            acc.free = [tok]
            add_to_stream(b, bk, tok)

        def add_to_stream(b, bk, tok):
            rows = xs[:, b * NT:(b + 1) * NT, :].rearrange("p t d -> p (t d)")
            DVE.wait(tok)
            tok = DVE.do(lambda e: e.tensor_tensor(rows, rows, bk.t[:, :], ALU.add), dve_acc)
            bk.free = [tok]
            xs_ready[b] = [tok]

        def value_range():
            DVE.wait(*attn_weights)
            tok = DVE.do(lambda e: e.tensor_reduce(v_max[:, :], f32(wqkvh[:, 2 * INNER:3 * INNER]), AX.X, ALU.max,
                                                   apply_absolute_value=True), dve_small)
            POOL.wait(tok)
            tok = POOL.do(lambda e: e.partition_all_reduce(v_top[:, :], v_max[:, :], P, bass.bass_isa.ReduceOp.max),
                          pool_small)
            DVE.wait(tok)
            tok = DVE.do(lambda e: e.tensor_scalar(v_max[:, :], v_top[:, :], 2.0 ** -100, 2.0 ** 100, ALU.max,
                                                   ALU.min), dve_small)
            DVE.wait(tok)
            tok = DVE.do(lambda e: e.tensor_scalar(v_pow[:, :].bitcast(U32), v_max[:, :].bitcast(U32), 0x7F800000,
                                                   None, ALU.bitwise_and), dve_small)
            DVE.wait(tok)
            tok = DVE.do(lambda e: e.reciprocal(v_inv[:, :], v_pow[:, :]), dve_small)
            DVE.wait(tok)
            DVE.do(lambda e: e.tensor_scalar(v_scale[:, :], v_inv[:, :], 8.0, None, ALU.mult), dve_small)
            return DVE.do(lambda e: e.tensor_scalar(pv_scale[:, :], v_inv[:, :], 8.0, P_SCALE, ALU.mult, ALU.mult),
                          dve_small)

        UNITS = [[(0, 3)], [(0, 2), (0, 0)], [(1, 3)], [(1, 2), (1, 0)], [(0, 1), (1, 1)]]
        SEGS = []
        for unit in UNITS:
            at, segs = 0, []
            for head, qt in unit:
                segs.append((head, qt, at))
                at += (qt + 1) * P
            SEGS.append(segs)
        NU = len(UNITS)

        def attention(b, xh, xl, scale_tok):
            qk_ready, probs_of, turned_of, o_last = {}, {}, {}, {}

            def project_v(t, half):
                cols = slice(half * 512, (half + 1) * 512)
                wide_cols = slice(2 * INNER + half * 512, 2 * INNER + (half + 1) * 512)
                s = slice(t * P, (t + 1) * P)
                bk = banks.take()
                PE.wait(*bk.free, *xh.ready, *attn_weights)
                tok = three_pass(bk.t[:, :], xh.t[:, s], xl.t[:, s], wqkvh[:, wide_cols], wqkvl[:, wide_cols], v_done)
                ACTQ.wait(scale_tok, *vh.free)
                DVE.wait(scale_tok, *vl.free)
                bk.free = split_bank(bk.t[:, :], vh.t[:, t, cols], vl.t[:, t, cols], [tok], v_scale[:, 0:1])
                return bk.free

            def project_qk(p):
                bufs = qk[p % 2]
                ready = []
                for k in range(2):
                    cols = slice(k * INNER + p * P, k * INNER + (p + 1) * P)
                    high, low = bufs[2 * k], bufs[2 * k + 1]
                    bk = banks.take()
                    PE.wait(*bk.free, *xh.ready, *attn_weights)
                    tok = three_pass(bk.t[:, :], wqkvh[:, cols], wqkvl[:, cols], xh.t[:, :], xl.t[:, :], qk_done)
                    ACTQ.wait(*high.free)
                    DVE.wait(*low.free)
                    bk.free = split_bank(bk.t[:, :], high.t[:, :], low.t[:, :], [tok],
                                         HEAD ** -0.5 if k == 0 else None)
                    ready += bk.free
                qk_ready[p] = ready

            def scores(n):
                p, u = divmod(n, NU)
                qh, ql, kh, kl = qk[p % 2]
                bk = banks.take()
                PE.wait(*bk.free, *qk_ready[p], consts)
                first_head, tok = SEGS[u][0][0], None
                for head, qt, at in SEGS[u]:
                    if head != first_head:
                        PE.wait(tok)
                    rows = slice(head * HEAD, (head + 1) * HEAD)
                    q, keys = slice(qt * P, (qt + 1) * P), slice(0, (qt + 1) * P)
                    three_pass(bk.t[:, at:at + (qt + 1) * P], qh.t[rows, q], ql.t[rows, q],
                               kh.t[rows, keys], kl.t[rows, keys], last=False)
                    tok = PE.do(lambda e, a=at + qt * P: e.matmul(bk.t[:, a:a + P], ident_b[:, :], causal[:, :],
                                                                  start=False, stop=True), scores_done)
                for buf in qk[p % 2]:
                    buf.free = [tok]
                pr = probs.take()
                ACTQ.wait(*pr.free)
                DVE.wait(tok)
                par = p % 2
                maxima = []
                if u == 0:
                    ACTQ.wait(*sums_free[par])
                for head, qt, at in SEGS[u]:
                    maxima.append(DVE.do(lambda e, h=head, q=qt, at=at: e.tensor_reduce(
                        neg_max[:, par, q, h:h + 1], bk.t[:, at:at + (q + 1) * P], AX.X, ALU.max, negate=True),
                        dve_max))
                ACTQ.wait(maxima[-1])
                for head, qt, at in SEGS[u]:
                    tok = ACTQ.do(lambda e, h=head, q=qt, at=at: e.activation(
                        pr.t[:, at:at + (q + 1) * P], bk.t[:, at:at + (q + 1) * P], ACT.Exp,
                        bias=neg_max[:, par, q, h:h + 1], accum_out=row_sum[:, par, q, h:h + 1]), act_exp)
                bk.free = [tok]
                probs_of[n] = (pr, tok)

            def turn(n):
                u = n % NU
                pr, tok = probs_of.pop(n)
                cols = sum((qt + 1) * P for _, qt, _ in SEGS[u])
                bk = banks.take()
                PE.wait(tok, *bk.free)
                for k in range(cols // P):
                    tok = PE.do(lambda e, k=k: e.transpose(bk.t[:, k * P:(k + 1) * P], pr.t[:, k * P:(k + 1) * P],
                                                           ident[:, :]), turned if k == cols // P - 1 else None)
                pr.free = [tok]
                th, tl = pTh.take(), pTl.take()
                ACTQ.wait(*th.free)
                DVE.wait(*tl.free)
                bk.free = split_bank(bk.t[:, 0:cols], th.t[:, 0:cols], tl.t[:, 0:cols], [tok], P_SCALE)
                turned_of[n] = (th, tl, bk.free)

            def weigh(n):
                p, u = divmod(n, NU)
                th, tl, ready = turned_of.pop(n)
                o = o_banks[p % 2]
                PE.wait(*ready, *v_ready)
                if u == 0:
                    PE.wait(*o.free)
                for head, qt, at in SEGS[u]:
                    dst = o.t[:, (qt * 2 + head) * HEAD:(qt * 2 + head + 1) * HEAD]
                    dims = slice(p * P + head * HEAD, p * P + (head + 1) * HEAD)
                    for kt in range(qt + 1):
                        blk = slice(at + kt * P, at + (kt + 1) * P)
                        tok = three_pass(dst, th.t[:, blk], tl.t[:, blk], vh.t[:, kt, dims], vl.t[:, kt, dims],
                                         pv_done if kt == qt else None, first=kt == 0, last=kt == qt)
                th.free = tl.free = [tok]
                o_last[p] = tok

            def finish_pair(p):
                par = p % 2
                o = o_banks[par]
                DVE.wait((act_exp, exp_of_pair[p]))
                tok = DVE.do(lambda e: e.tensor_scalar(scaled_sum[:, par], row_sum[:, par], pv_scale[:, 0:1], None,
                                                       ALU.mult), dve_small)
                sums_free[par] = [tok]
                DVE.wait(tok)
                tok = DVE.do(lambda e: e.reciprocal(inv_sum[:, par], scaled_sum[:, par]), dve_small)
                DVE.wait(tok, o_last[p], *attn.free)
                tok = DVE.do(lambda e: e.tensor_tensor(
                    attn.t[:, :, :].rearrange("p q (h d) -> p (q h) d", h=2),
                    o.t[:, :].rearrange("p (s d) -> p s d", d=HEAD),
                    inv_sum[:, par].rearrange("p q h -> p (q h)").unsqueeze(2).broadcast_to([P, NT * 2, HEAD]),
                    ALU.mult), dve_acc)
                o.free = [tok]
                bk = banks.take()
                PE.wait(tok, *bk.free)
                for t in range(NT):
                    tok = PE.do(lambda e, t=t: e.transpose(bk.t[:, t * P:(t + 1) * P], attn.t[:, t, :], ident[:, :]),
                                turned if t == NT - 1 else None)
                attn.free = [tok]
                ACTQ.wait(*aTh.free)
                DVE.wait(*aTl.free)
                bk.free = split_bank(bk.t[:, :], aTh.t[:, :], aTl.t[:, :], [tok])
                aTh.ready = bk.free

            def project_out(p):
                PE.wait(*aTh.ready)
                if p == 0:
                    PE.wait(*y_bank.free)
                tok = three_pass(y_bank.t[:, :], woh[:, p, :], wol[:, p, :], aTh.t[:, :], aTl.t[:, :], y_done,
                                 first=p == 0, last=p == PAIRS - 1)
                aTh.free = aTl.free = [tok]
                return tok

            v_ready = []
            exp_of_pair = {}
            project_qk(0)
            for t in range(NT):
                for half in range(INNER // 512):
                    v_ready += project_v(t, half)
            tail = {}
            for n in range(NU * PAIRS + 5):
                if n % NU == 2 and n // NU + 1 < PAIRS:
                    project_qk(n // NU + 1)
                if n < NU * PAIRS:
                    scores(n)
                    exp_of_pair[n // NU] = act_exp.value
                if 1 <= n <= NU * PAIRS:
                    turn(n - 1)
                if 2 <= n <= NU * PAIRS + 1:
                    weigh(n - 2)
                m = n - 2
                if m >= 0 and m % NU == NU - 1 and m // NU < PAIRS:
                    finish_pair(m // NU)
                m = n - 4
                if m >= 0 and m % NU == NU - 1 and m // NU < PAIRS:
                    tok = project_out(m // NU)
                yield
            vh.free = vl.free = [(pv_done, pv_done.value)]
            xh.free = xl.free = [(qk_done, qk_done.value), (v_done, v_done.value)]
            yT = attn.t[:, :, :].rearrange("p t d -> p (t d)")
            ACTQ.wait(tok, *attn.free)
            tok = ACTQ.do(lambda e: e.activation(yT[:, :], y_bank.t[:, :], ACT.Copy), act_copy)
            y_bank.free = [tok]
            bk = banks.take()
            PE.wait(tok, *bk.free)
            for t in range(NT):
                tok = PE.do(lambda e, t=t: e.transpose(bk.t[:, t * P:(t + 1) * P], yT[:, t * P:(t + 1) * P],
                                                       ident[:, :]), turned if t == NT - 1 else None)
            attn.free = [tok]
            add_to_stream(b, bk, tok)

        sums_free = [[], []]

        ORDER = [("ff1", 0), ("ff1", 1), ("att", 0), ("ff1", 2), ("att", 1), ("ff2", 0), ("ff1", 3), ("att", 2),
                 ("ff2", 1), ("att", 3), ("ff2", 2), ("ff2", 3)]
        for b in range(B):
            if b > 0:
                x_tok.append(SP.do(lambda e, b=b: e.dma_start(xs[:, b * NT:(b + 1) * NT, :], chunk_of(x, b)),
                                   x_in[b], 16))
            xs_ready[b] = [x_tok[b]]
        scale_tok = None
        normed = layer_norm(0)
        for pos, (kind, b) in enumerate(ORDER):
            xh, xl = normed
            if kind == "att":
                if scale_tok is None:
                    scale_tok = value_range()
                    vh.free, vl.free = raw_free[0] + raw_free[1], raw_free[0] + raw_free[1]
                    for i in range(2):
                        probs.buffers[i].free = raw_w_free[i]
                layer = attention(b, xh, xl, scale_tok)
            else:
                layer = feed_forward(pos, b, xh, xl, prepare=pos == 0)
            steps = 0
            for _ in layer:
                steps += 1
                if pos == 0 and steps % 3 == 0 and steps // 3 <= len(wide_weights):
                    load_attention_weight(steps // 3 - 1)
                if steps == 16 and pos + 1 < len(ORDER):
                    nxt, nb = ORDER[pos + 1]
                    normed = layer_norm(nb)
                    if nxt != "att":
                        router(pos + 1, nb, *normed)
            if kind == "ff2":
                SP.wait(*xs_ready[b])
                last = SP.do(lambda e, b=b: e.dma_start(chunk_of(out, b), xs[:, b * NT:(b + 1) * NT, :]), stored, 16)
        SP.wait(last, (route_stored, route_stored.value))

        block = ctx.enter_context(nc.Block())
        block.sync(SP.play)
        block.gpsimd(POOL.play)
        block.tensor(PE.play)
        block.scalar(ACTQ.play)
        block.vector(DVE.play)


_INS = ["L0_attn_inputs", "L0_attn_W_qkv", "L0_attn_W_out", "L0_ffn_Wg", "L0_ffn_routing_bias", "L0_ffn_W1",
        "L0_ffn_W2", "L0_ffn_W3", "L0_ffn_Ws1", "L0_ffn_Ws2", "L0_ffn_Ws3"]


def kernel(**inputs):
    import numpy as np
    import concourse.bacc as bacc
    from concourse.bass_utils import run_bass_kernel_spmd

    nc = bacc.Bacc("TRN2", target_bir_lowering=False, num_devices=1)
    arrays, args = {}, []
    for name in _INS:
        a = np.ascontiguousarray(inputs[name])
        arrays[f"in_{name}"] = a
        args.append(nc.dram_tensor(f"in_{name}", a.shape, mybir.dt.from_np(a.dtype), kind="ExternalInput").ap())
    shape = inputs["L0_attn_inputs"].shape
    out = nc.dram_tensor("out", shape, F32, kind="ExternalOutput").ap()
    experts = inputs["L0_ffn_Wg"].shape[0]
    tiles = shape[1] // P
    scratch = nc.dram_tensor("weight_scratch", (3 * shape[0], tiles * experts, P), F32, kind="Internal").ap()
    macaron(nc, *args, out, scratch)
    result = run_bass_kernel_spmd(nc, [arrays], core_ids=[0])
    return result.results[0]["out"]
```

```python
from contextlib import ExitStack

import concourse.bass as bass
from concourse import mybir

F32 = mybir.dt.float32
F32R = mybir.dt.float32r
F16 = mybir.dt.float16
BF16 = mybir.dt.bfloat16
U32 = mybir.dt.uint32
ALU = mybir.AluOpType
ACT = mybir.ActivationFunctionType
AX = mybir.AxisListType

P = 128
LN_EPS = 1e-5
TOP_K = 4
ENDING = 2
MASKED = -8e30
P_SCALE = 4096.0


class Signal:

    def __init__(self, sem):
        self.sem, self.value = sem, 0


class Queue:

    def __init__(self):
        self.steps, self.passed = [], {}

    def wait(self, *tokens):
        for signal, value in tokens:
            if self.passed.get(signal, 0) < value:
                self.passed[signal] = value
                self.steps.append(lambda eng, s=signal.sem, v=value: eng.wait_ge(s, v))

    def do(self, issue, signal=None, by=1):
        if signal is None:
            self.steps.append(issue)
            return None
        self.steps.append(lambda eng: issue(eng).then_inc(signal.sem, by))
        signal.value += by
        return signal, signal.value

    def play(self, eng):
        for step in self.steps:
            step(eng)


class Buffer:

    def __init__(self, tensor):
        self.t, self.free, self.ready = tensor, [], []


class Ring:
    def __init__(self, buffers):
        self.buffers, self.taken = buffers, 0

    def take(self):
        self.taken += 1
        return self.buffers[(self.taken - 1) % len(self.buffers)]


def macaron(nc, x, w_qkv, w_out, w_gate, routing_bias, w1, w2, w3, ws1, ws2, ws3, out, weight_scratch):
    B, L, D = x.shape
    E, HID, _ = w1.shape
    NE = E + 1
    NT = L // P
    INNER = w_out.shape[0]
    HEAD = 64
    PAIRS = INNER // P
    TILES = [(j * P, min(P, HID - j * P)) for j in range((HID + P - 1) // P)]
    NJ = len(TILES)
    assert D == P and L == 512 and NJ == 3 and 2 * HEAD == P

    with ExitStack() as ctx:
        def sb(name, shape, dt=F32):
            return ctx.enter_context(nc.sbuf_tensor(name, shape, dt))

        def bank(name):
            return Buffer(ctx.enter_context(nc.psum_tensor(name, [P, 512], F32)))

        def signal(name):
            return Signal(ctx.enter_context(nc.semaphore(name)))

        w1h, w1l = sb("w1h", [P, NE, HID], F32R), sb("w1l", [P, NE, HID], F32R)
        w2h, w2l = sb("w2h", [P, NE, HID], F32R), sb("w2l", [P, NE, HID], F32R)
        w3h, w3l = sb("w3h", [P, NE, NJ, D], F32R), sb("w3l", [P, NE, NJ, D], F32R)
        wqkvh, wqkvl = sb("wqkvh", [P, 3 * INNER], F32R), sb("wqkvl", [P, 3 * INNER], F32R)
        woh, wol = sb("woh", [P, PAIRS, D], F32R), sb("wol", [P, PAIRS, D], F32R)
        wgh, wgl = sb("wgh", [P, E], F32R), sb("wgl", [P, E], F32R)

        ident = sb("ident", [P, P])
        ident_b = sb("ident_b", [P, P], BF16)
        causal = sb("causal", [P, P], BF16)
        earlier = sb("earlier", [P, E, E])
        neg_half = sb("neg_half", [P, NT])
        bias_b = sb("bias_b", [P, E])
        v_max = sb("v_max", [P, 1])
        v_top = sb("v_top", [P, 1])
        v_pow = sb("v_pow", [P, 1])
        v_inv = sb("v_inv", [P, 1])
        v_scale = sb("v_scale", [P, 1])
        pv_scale = sb("pv_scale", [P, 1])

        xs = sb("xs", [P, B * NT, D])
        xs_ready = [[] for _ in range(B)]
        xn = Buffer(sb("xn", [P, NT, D]))
        stats = sb("stats", [P, NT, 6])
        moments = sb("moments", [P, NT, 2])
        var_eps = sb("var_eps", [P, NT])
        rstd = sb("rstd", [P, NT])
        xnT = Ring([(Buffer(sb(f"xnTh{i}", [P, L], F32R)), Buffer(sb(f"xnTl{i}", [P, L], F32R))) for i in range(2)])

        gate = sb("gate", [P, NT, E])
        top = sb("top", [P, NT])
        beats, ties = [xn.t[:, :, :].rearrange("p t d -> p (t d)")[:, k * NT * E * E:(k + 1) * NT * E * E]
                       .rearrange("p (t i j) -> p t i j", t=NT, i=E) for k in range(2)]
        rank = sb("rank", [P, NT, E])
        shifted = sb("shifted", [P, NT, E])
        expo = sb("expo", [P, NT, E])
        chosen = sb("chosen", [P, NT, E])
        total = sb("total", [P, NT])
        inv_total = sb("inv_total", [P, NT])
        route = Buffer(sb("route", [P, NT, E]))
        routeT = Buffer(sb("routeT", [NT * E, P]))
        wide = Ring([Buffer(sb(f"wide{i}", [P, NT, P])) for i in range(2)])

        silu = Ring([Buffer(sb(f"silu{i}", [P, L])) for i in range(2)])
        glu = Ring([Buffer(sb(f"glu{i}", [P, L])) for i in range(2)])
        gluh = Ring([Buffer(sb(f"gluh{i}", [P, L], F32R)) for i in range(3)])
        glul = Ring([Buffer(sb(f"glul{i}", [P, L], F32R)) for i in range(3)])
        acc = Buffer(sb("acc", [P, L]))
        part = Buffer(sb("part", [P, L]))

        qk = [[Buffer(sb(f"{n}{i}", [P, L], F32R)) for n in ("qh", "ql", "kh", "kl")] for i in range(2)]
        vh, vl = Buffer(sb("vh", [P, NT, INNER], F16)), Buffer(sb("vl", [P, NT, INNER], F16))
        probs = Ring([Buffer(sb(f"probs{i}", [P, 512])) for i in range(3)])
        pTh = Ring([Buffer(sb(f"pTh{i}", [P, 512], F16)) for i in range(3)])
        pTl = Ring([Buffer(sb(f"pTl{i}", [P, 512], F16)) for i in range(3)])
        neg_max = sb("neg_max", [P, 2, NT, 2])
        row_sum = sb("row_sum", [P, 2, NT, 2])
        scaled_sum = sb("scaled_sum", [P, 2, NT, 2])
        inv_sum = sb("inv_sum", [P, 2, NT, 2])
        attn = Buffer(sb("attn", [P, NT, P]))
        aTh, aTl = Buffer(sb("aTh", [P, L], F32R)), Buffer(sb("aTl", [P, L], F32R))
        raw12 = [vh.t[:, :, :].rearrange("p t n -> p (t n)")[:, i * 1536:(i + 1) * 1536].bitcast(F32)
                 .rearrange("p (w j d) -> p w j d", w=2, j=3) for i in range(2)]
        raw3 = [vl.t[:, :, :].rearrange("p t n -> p (t n)")[:, i * 1024:i * 1024 + 2 * HID].bitcast(F32)
                for i in range(2)]
        raw_w = [probs.buffers[i].t[:, :] for i in range(2)]

        banks = Ring([bank(f"bank{i}") for i in range(5)])
        sum_bank = bank("sum_bank")
        o_banks = [bank("o_bank0"), bank("o_bank1")]

        x_in = [signal(f"x_in{b}") for b in range(B)]
        small_in = signal("small_in")
        raw_in = [signal(f"raw_in{i}") for i in range(2)]
        raw_w_in = [signal(f"raw_w_in{i}") for i in range(2)]
        route_stored = signal("route_stored")
        wide_in = [signal(f"wide_in{i}") for i in range(2)]
        stored = signal("stored")
        consts_made = signal("consts_made")
        pool_split = signal("pool_split")
        pool_small = signal("pool_small")
        turned = signal("turned")
        hidden_done = signal("hidden_done")
        down_done = signal("down_done")
        gate_done = signal("gate_done")
        qk_done = signal("qk_done")
        v_done = signal("v_done")
        scores_done = signal("scores_done")
        pv_done = signal("pv_done")
        y_done = signal("y_done")
        act_high = signal("act_high")
        act_silu = signal("act_silu")
        act_exp = signal("act_exp")
        act_copy = signal("act_copy")
        dve_low = signal("dve_low")
        dve_glu = signal("dve_glu")
        dve_acc = signal("dve_acc")
        dve_small = signal("dve_small")
        dve_max = signal("dve_max")

        SP, POOL, PE, ACTQ, DVE = Queue(), Queue(), Queue(), Queue(), Queue()

        def f32(ap):
            return ap.bitcast(F32)

        chunk_of = lambda t, b: t[b].rearrange("(t p) d -> p t d", p=P)
        x_tok = [SP.do(lambda e, b=b: e.dma_start(xs[:, b * NT:(b + 1) * NT, :], chunk_of(x, b)), x_in[b], 16)
                 for b in range(1)]
        wg_raw = attn.t[0:E, 0, :]
        SP.do(lambda e: e.dma_start(wg_raw, w_gate), small_in, 16)
        small_tok = SP.do(lambda e: e.dma_start(bias_b[:, :], routing_bias.rearrange("(a n) -> a n", a=1)
                                                .broadcast_to([P, E])), small_in, 16)

        raw_free = [[], []]
        raw_ready = {}

        def load_expert(n):
            i = n % 2
            SP.wait(*raw_free[i])
            srcs = [ws1, ws2] if n == 0 else [w1[n - 1], w2[n - 1]]
            for k, src in enumerate(srcs):
                SP.do(lambda e, k=k, src=src: e.dma_start(
                    raw12[i][:, k, 0:2, :], src[0:2 * P, :].rearrange("(j p) d -> p j d", p=P)), raw_in[i], 16)
                SP.do(lambda e, k=k, src=src: e.dma_start(raw12[i][0:HID - 2 * P, k, 2, :], src[2 * P:HID, :]),
                      raw_in[i], 16)
            raw_ready[n] = SP.do(lambda e: e.dma_start(raw3[i], ws3 if n == 0 else w3[n - 1]), raw_in[i], 16)

        raw_w_free = [[], []]
        wide_weights = [(w_qkv[:, c * 512:(c + 1) * 512], wqkvh[:, c * 512:(c + 1) * 512],
                         wqkvl[:, c * 512:(c + 1) * 512]) for c in range(3 * INNER // 512)]
        wide_weights += [(w_out.rearrange("(k p) d -> p k d", p=P)[:, 4 * c:4 * c + 4, :],
                          woh[:, 4 * c:4 * c + 4, :], wol[:, 4 * c:4 * c + 4, :]) for c in range(PAIRS // 4)]
        attn_weights = []

        def load_attention_weight(c):
            src, high, low = wide_weights[c]
            i = c % 2
            raw = raw_w[i] if c < 3 * INNER // 512 else raw_w[i].rearrange("p (k d) -> p k d", k=4)
            SP.wait(*raw_w_free[i])
            tok = SP.do(lambda e: e.dma_start(raw, src), raw_w_in[i], 16)
            POOL.wait(tok)
            tok = POOL.do(lambda e: e.tensor_copy(high, raw), pool_split)
            POOL.wait(tok)
            tok = POOL.do(lambda e: e.tensor_tensor(low, raw, f32(high), ALU.subtract), pool_split)
            raw_w_free[i] = [tok]
            attn_weights.append(tok)

        POOL.do(lambda e: e.memset(ident[:, :], 0.0), consts_made)
        POOL.do(lambda e: e.memset(causal[:, :], 0.0), consts_made)
        POOL.do(lambda e: e.memset(earlier[:, :, :], 1.0), consts_made)
        tok = POOL.do(lambda e: e.memset(neg_half[:, :], -0.5), consts_made)
        POOL.wait(tok)
        tok = POOL.do(lambda e: e.affine_select(out=ident[:, :], in_=ident[:, :], compare_op=ALU.not_equal, fill=1.0,
                                                base=0, pattern=[[-1, P]], channel_multiplier=1), consts_made)
        POOL.do(lambda e: e.affine_select(out=causal[:, :], in_=causal[:, :], compare_op=ALU.is_ge, fill=MASKED,
                                          base=0, pattern=[[-1, P]], channel_multiplier=1), consts_made)
        POOL.do(lambda e: e.affine_select(out=earlier[:, :, :], in_=earlier[:, :, :], compare_op=ALU.is_gt, fill=0.0,
                                          base=0, pattern=[[1, E], [-1, E]], channel_multiplier=0), consts_made)
        POOL.wait(tok)
        consts = POOL.do(lambda e: e.tensor_copy(ident_b[:, :], ident[:, :]), consts_made)

        bk = banks.take()
        PE.wait(consts, small_tok)
        tok = PE.do(lambda e: e.transpose(bk.t[:, 0:E], wg_raw, ident[0:E, 0:E]), turned)
        attn.free = [tok]
        ACTQ.wait(tok)
        tok = ACTQ.do(lambda e: e.activation(wgh[:, :], bk.t[:, 0:E], ACT.Copy), act_high)
        DVE.wait(tok)
        gate_weights = DVE.do(lambda e: e.tensor_tensor(wgl[:, :], bk.t[:, 0:E], f32(wgh[:, :]), ALU.subtract), dve_low)
        bk.free = [gate_weights]

        def split_bank(src, high, low, after, scale=None):
            ACTQ.wait(*after)
            t_high = ACTQ.do(lambda e: e.activation(high, src, ACT.Copy, scale=1.0 if scale is None else scale),
                             act_high)
            DVE.wait(t_high)
            hv = f32(high) if high.dtype == F32R else high
            if scale is None:
                t_low = DVE.do(lambda e: e.tensor_tensor(low, src, hv, ALU.subtract), dve_low)
            else:
                t_low = DVE.do(lambda e: e.scalar_tensor_tensor(low, src, scale, hv, ALU.mult, ALU.subtract), dve_low)
            return [t_high, t_low]

        expert_ready = {}

        def prepare_expert(n):
            i = n % 2
            PE.wait(raw_ready[n])
            ready = []
            for k, (high, low) in enumerate(((w1h, w1l), (w2h, w2l))):
                bk = banks.take()
                PE.wait(*bk.free)
                for j, (h0, m) in enumerate(TILES):
                    last = j == NJ - 1
                    tok = PE.do(lambda e, j=j, h0=h0, m=m, k=k, bk=bk: e.transpose(
                        bk.t[:, h0:h0 + m], raw12[i][0:m, k, j, :], ident[0:m, 0:m]), turned if last else None)
                bk.free = split_bank(bk.t[:, 0:HID], high[:, n, :], low[:, n, :], [tok])
                ready += bk.free
            bk = banks.take()
            PE.wait(*bk.free)
            for j, (h0, m) in enumerate(TILES):
                tok = PE.do(lambda e, j=j, h0=h0, m=m, bk=bk: e.transpose(
                    bk.t[0:m, j * D:(j + 1) * D], raw3[i][:, h0:h0 + m], ident[:, :]),
                    turned if j == NJ - 1 else None)
            raw_free[i] = [tok]
            m = TILES[-1][1]
            both = split_bank(bk.t[:, 0:2 * D], w3h[:, n, 0:2, :].rearrange("p j d -> p (j d)"),
                              w3l[:, n, 0:2, :].rearrange("p j d -> p (j d)"), [tok])
            DVE.wait(both[0])
            tail = split_bank(bk.t[0:m, 2 * D:3 * D], w3h[0:m, n, 2, :], w3l[0:m, n, 2, :], [tok, both[1]])
            bk.free = tail
            expert_ready[n] = ready + both + tail

        def three_pass(ps, high, low, mhigh, mlow, signal=None, first=True, last=True):
            PE.do(lambda e: e.matmul(ps, high, mhigh, start=first, stop=False))
            PE.do(lambda e: e.matmul(ps, high, mlow, start=False, stop=False))
            return PE.do(lambda e: e.matmul(ps, low, mhigh, start=False, stop=last), signal)

        def layer_norm(b, halves):
            rows = [xs[:, b * NT + t, :] for t in range(NT)]
            DVE.wait(*xs_ready[b])
            for t in range(NT):
                tok = DVE.do(lambda e, t=t: e.bn_stats(stats[:, t, :], rows[t]), dve_small)
            DVE.wait(tok)
            for t in range(NT):
                tok = DVE.do(lambda e, t=t: e.bn_aggr(moments[:, t, :], stats[:, t, :]), dve_small)
            DVE.wait(tok)
            tok = DVE.do(lambda e: e.tensor_scalar(var_eps[:, :], moments[:, :, 1], LN_EPS, None, ALU.add), dve_small)
            POOL.wait(tok, consts)
            tok = POOL.do(lambda e: e.tensor_tensor(rstd[:, :], var_eps[:, :], neg_half[:, :], ALU.pow), pool_small)
            DVE.wait(tok, *xn.free)
            for t in range(NT):
                tok = DVE.do(lambda e, t=t: e.tensor_scalar(xn.t[:, t, :], rows[t], moments[:, t, 0:1],
                                                            rstd[:, t:t + 1], ALU.subtract, ALU.mult), dve_small)
            yield
            bk = banks.take()
            PE.wait(tok, *bk.free)
            for t in range(NT):
                tok = PE.do(lambda e, t=t: e.transpose(bk.t[:, t * P:(t + 1) * P], xn.t[:, t, :], ident[:, :]),
                            turned if t == NT - 1 else None)
            xn.free = [tok]
            xh, xl = halves
            ACTQ.wait(*xh.free)
            DVE.wait(*xl.free)
            bk.free = split_bank(bk.t[:, :], xh.t[:, :], xl.t[:, :], [tok])
            xh.ready = xl.ready = bk.free

        scratch_ready = {}

        def router(c, b, xh, xl):
            bk = banks.take()
            PE.wait(*bk.free, *xh.ready, gate_weights)
            for t in range(NT):
                s = slice(t * P, (t + 1) * P)
                tok = three_pass(bk.t[:, t * E:(t + 1) * E], xh.t[:, s], xl.t[:, s], wgh[:, :], wgl[:, :],
                                 gate_done if t == NT - 1 else None)
            rows_i = lambda a: a[:, :, :].unsqueeze(3).broadcast_to([P, NT, E, E])
            rows_j = lambda a: a[:, :, :].unsqueeze(2).broadcast_to([P, NT, E, E])
            over = lambda a: a[:, :].unsqueeze(2).broadcast_to([P, NT, E])

            def small(issue, *waits):
                DVE.wait(*waits)
                return DVE.do(issue, dve_small)

            tok = small(lambda e: e.tensor_tensor(gate[:, :, :], bk.t[:, 0:NT * E].rearrange("p (t n) -> p t n", t=NT),
                                                  bias_b[:, :].unsqueeze(1).broadcast_to([P, NT, E]), ALU.add),
                        tok, small_tok)
            bk.free = [tok]
            t_top = small(lambda e: e.tensor_reduce(top[:, :], gate[:, :, :], AX.X, ALU.max), tok)
            small(lambda e: e.tensor_tensor(beats, rows_j(gate), rows_i(gate), ALU.is_gt))
            tok = small(lambda e: e.tensor_tensor(ties, rows_j(gate), rows_i(gate), ALU.is_equal))
            t_shift = small(lambda e: e.tensor_tensor(shifted[:, :, :], gate[:, :, :], over(top), ALU.subtract), t_top)
            tok = small(lambda e: e.tensor_tensor(ties, ties,
                                                  earlier[:, :, :].unsqueeze(1).broadcast_to([P, NT, E, E]), ALU.mult),
                        tok, consts)
            ACTQ.wait(t_shift)
            t_exp = ACTQ.do(lambda e: e.activation(expo[:, :, :], shifted[:, :, :], ACT.Exp), act_exp)
            tok = small(lambda e: e.tensor_tensor(beats, beats, ties, ALU.add), tok)
            tok = small(lambda e: e.tensor_reduce(rank[:, :, :], beats, AX.X, ALU.add), tok)
            tok = small(lambda e: e.scalar_tensor_tensor(chosen[:, :, :], rank[:, :, :], float(TOP_K), expo[:, :, :],
                                                         ALU.is_lt, ALU.mult), tok, t_exp)
            tok = small(lambda e: e.tensor_reduce(total[:, :], chosen[:, :, :], AX.X, ALU.add), tok)
            tok = small(lambda e: e.reciprocal(inv_total[:, :], total[:, :]), tok)
            tok = small(lambda e: e.scalar_tensor_tensor(route.t[:, :, :], chosen[:, :, :], 0.5, over(inv_total),
                                                         ALU.mult, ALU.mult), tok, *route.free)
            yield
            bt = banks.take()
            PE.wait(tok, *bt.free)
            tok = PE.do(lambda e: e.transpose(bt.t[0:NT * E, 0:P], route.t[:, :, :].rearrange("p t n -> p (t n)"),
                                              ident[:, :]), turned)
            route.free = [tok]
            DVE.wait(tok, *routeT.free)
            tok = DVE.do(lambda e: e.tensor_copy(routeT.t[:, :], bt.t[0:NT * E, 0:P]), dve_small)
            bt.free = [tok]
            SP.wait(tok)
            tok = SP.do(lambda e: e.dma_start(weight_scratch[c], routeT.t[:, :]), route_stored, 16)
            routeT.free = [tok]
            scratch_ready[c] = tok

        def widen(c, e_n):
            n = wide.taken % 2
            buf = wide.take()
            SP.wait(scratch_ready[c], *buf.free)
            src = weight_scratch[c].rearrange("(t n) p -> n t p", t=NT)[e_n:e_n + 1].broadcast_to([P, NT, P])
            buf.ready = [SP.do(lambda e: e.dma_start(buf.t[:, :, :], src), wide_in[n], 16)]
            return buf

        def feed_forward(c, b, xh, xl, prepare):
            work = [(n, j) for n in range(NE) for j in range(NJ)]
            tiles = {}
            if prepare:
                load_expert(0)
                load_expert(1)
                prepare_expert(0)
                yield from router(c, b, xh, xl)

            def hidden(i):
                n, j = work[i]
                h0, m = TILES[j]
                b1, b2 = banks.take(), banks.take()
                PE.wait(*b1.free, *xh.ready, *expert_ready[n])
                t1 = three_pass(b1.t[0:m, :], w1h[:, n, h0:h0 + m], w1l[:, n, h0:h0 + m], xh.t[:, :], xl.t[:, :],
                                hidden_done)
                PE.wait(*b2.free)
                t2 = three_pass(b2.t[0:m, :], w2h[:, n, h0:h0 + m], w2l[:, n, h0:h0 + m], xh.t[:, :], xl.t[:, :],
                                hidden_done)
                s, g, gh, gl = silu.take(), glu.take(), gluh.take(), glul.take()
                ACTQ.wait(t1, *s.free)
                ts = ACTQ.do(lambda e: e.activation(s.t[0:m, :], b1.t[0:m, :], ACT.Silu), act_silu)
                b1.free = [ts]
                DVE.wait(t2, ts, *g.free)
                tg = DVE.do(lambda e: e.tensor_tensor(g.t[0:m, :], s.t[0:m, :], b2.t[0:m, :], ALU.mult), dve_glu)
                b2.free = s.free = [tg]
                ACTQ.wait(tg, *gh.free)
                th = ACTQ.do(lambda e: e.activation(gh.t[0:m, :], g.t[0:m, :], ACT.Copy), act_high)
                POOL.wait(th, tg, *gl.free)
                tl = POOL.do(lambda e: e.tensor_tensor(gl.t[0:m, :], g.t[0:m, :], f32(gh.t[0:m, :]), ALU.subtract),
                             pool_split)
                g.free = [th, tl]
                tiles[i] = (gh, gl, [th, tl])

            def down(i):
                n, j = work[i]
                m = TILES[j][1]
                gh, gl, ready = tiles.pop(i)
                PE.wait(*ready)
                if j == 0:
                    PE.wait(*sum_bank.free)
                tok = three_pass(sum_bank.t[:, :], w3h[0:m, n, j, :], w3l[0:m, n, j, :], gh.t[0:m, :], gl.t[0:m, :],
                                 down_done, first=j == 0, last=j == NJ - 1)
                gh.free = gl.free = [tok]
                if j < NJ - 1:
                    return
                if n == 0:
                    DVE.wait(tok, *acc.free)
                    tok = DVE.do(lambda e: e.tensor_scalar(acc.t[:, :], sum_bank.t[:, :], 0.5, None, ALU.mult),
                                 dve_acc)
                    sum_bank.free = acc.ready = [tok]
                    return
                w = wides.pop(n)
                DVE.wait(tok, *w.ready, *part.free)
                tok = DVE.do(lambda e: e.tensor_tensor(part.t[:, :], sum_bank.t[:, :],
                                                       w.t[:, :, :].rearrange("p t n -> p (t n)"), ALU.mult), dve_acc)
                w.free = sum_bank.free = [tok]
                DVE.wait(tok, *acc.ready)
                tok = DVE.do(lambda e: e.tensor_tensor(acc.t[:, :], acc.t[:, :], part.t[:, :], ALU.add), dve_acc)
                part.free = acc.ready = [tok]

            wides = {}
            LAG = 2
            for i in range(len(work) + LAG):
                if i < len(work):
                    n, j = work[i]
                    if j == 0 and n + 1 < NE and prepare:
                        prepare_expert(n + 1)
                        if n + 2 < NE:
                            load_expert(n + 2)
                    hidden(i)
                if i >= LAG:
                    down(i - LAG)
                if i < len(work) and j == NJ - 1 and n + 1 < NE:
                    wides[n + 1] = widen(c, n)
                yield i >= len(work) - 1
                if i == len(work) - 1:
                    xh.free = xl.free = [(hidden_done, hidden_done.value)]
            yield True
            bk = banks.take()
            PE.wait(*acc.ready, *bk.free)
            for t in range(NT):
                tok = PE.do(lambda e, t=t: e.transpose(bk.t[:, t * P:(t + 1) * P], acc.t[:, t * P:(t + 1) * P],
                                                       ident[:, :]), turned if t == NT - 1 else None)
            acc.free = [tok]
            add_to_stream(b, bk, tok)

        def add_to_stream(b, bk, tok):
            rows = xs[:, b * NT:(b + 1) * NT, :].rearrange("p t d -> p (t d)")
            DVE.wait(tok)
            tok = DVE.do(lambda e: e.tensor_tensor(rows, rows, bk.t[:, :], ALU.add), dve_acc)
            bk.free = [tok]
            xs_ready[b] = [tok]

        def value_range():
            DVE.wait(*attn_weights)
            tok = DVE.do(lambda e: e.tensor_reduce(v_max[:, :], f32(wqkvh[:, 2 * INNER:3 * INNER]), AX.X, ALU.max,
                                                   apply_absolute_value=True), dve_small)
            POOL.wait(tok)
            tok = POOL.do(lambda e: e.partition_all_reduce(v_top[:, :], v_max[:, :], P, bass.bass_isa.ReduceOp.max),
                          pool_small)
            DVE.wait(tok)
            tok = DVE.do(lambda e: e.tensor_scalar(v_max[:, :], v_top[:, :], 2.0 ** -100, 2.0 ** 100, ALU.max,
                                                   ALU.min), dve_small)
            DVE.wait(tok)
            tok = DVE.do(lambda e: e.tensor_scalar(v_pow[:, :].bitcast(U32), v_max[:, :].bitcast(U32), 0x7F800000,
                                                   None, ALU.bitwise_and), dve_small)
            DVE.wait(tok)
            tok = DVE.do(lambda e: e.reciprocal(v_inv[:, :], v_pow[:, :]), dve_small)
            DVE.wait(tok)
            DVE.do(lambda e: e.tensor_scalar(v_scale[:, :], v_inv[:, :], 8.0, None, ALU.mult), dve_small)
            return DVE.do(lambda e: e.tensor_scalar(pv_scale[:, :], v_inv[:, :], 8.0, P_SCALE, ALU.mult, ALU.mult),
                          dve_small)

        UNITS = [[(0, 3)], [(0, 2), (0, 0)], [(1, 3)], [(1, 2), (1, 0)], [(0, 1), (1, 1)]]
        SEGS = []
        for unit in UNITS:
            at, segs = 0, []
            for head, qt in unit:
                segs.append((head, qt, at))
                at += (qt + 1) * P
            SEGS.append(segs)
        NU = len(UNITS)

        def attention(b, xh, xl, scale_tok):
            qk_ready, scored, probs_of, turned_of, o_last = {}, {}, {}, {}, {}

            def project_v(t, half):
                cols = slice(half * 512, (half + 1) * 512)
                wide_cols = slice(2 * INNER + half * 512, 2 * INNER + (half + 1) * 512)
                s = slice(t * P, (t + 1) * P)
                bk = banks.take()
                PE.wait(*bk.free, *xh.ready, *attn_weights)
                tok = three_pass(bk.t[:, :], xh.t[:, s], xl.t[:, s], wqkvh[:, wide_cols], wqkvl[:, wide_cols], v_done)
                ACTQ.wait(scale_tok, *vh.free)
                DVE.wait(scale_tok, *vl.free)
                bk.free = split_bank(bk.t[:, :], vh.t[:, t, cols], vl.t[:, t, cols], [tok], v_scale[:, 0:1])
                return bk.free

            def project_qk(p):
                bufs = qk[p % 2]
                ready = []
                for k in range(2):
                    cols = slice(k * INNER + p * P, k * INNER + (p + 1) * P)
                    high, low = bufs[2 * k], bufs[2 * k + 1]
                    bk = banks.take()
                    PE.wait(*bk.free, *xh.ready, *attn_weights)
                    tok = three_pass(bk.t[:, :], wqkvh[:, cols], wqkvl[:, cols], xh.t[:, :], xl.t[:, :], qk_done)
                    ACTQ.wait(*high.free)
                    DVE.wait(*low.free)
                    bk.free = split_bank(bk.t[:, :], high.t[:, :], low.t[:, :], [tok],
                                         HEAD ** -0.5 if k == 0 else None)
                    ready += bk.free
                qk_ready[p] = ready

            def scores(n):
                p, u = divmod(n, NU)
                qh, ql, kh, kl = qk[p % 2]
                bk = banks.take()
                PE.wait(*bk.free, *qk_ready[p], consts)
                first_head, tok = SEGS[u][0][0], None
                for head, qt, at in SEGS[u]:
                    if head != first_head:
                        PE.wait(tok)
                    rows = slice(head * HEAD, (head + 1) * HEAD)
                    q, keys = slice(qt * P, (qt + 1) * P), slice(0, (qt + 1) * P)
                    three_pass(bk.t[:, at:at + (qt + 1) * P], qh.t[rows, q], ql.t[rows, q],
                               kh.t[rows, keys], kl.t[rows, keys], last=False)
                    tok = PE.do(lambda e, a=at + qt * P: e.matmul(bk.t[:, a:a + P], ident_b[:, :], causal[:, :],
                                                                  start=False, stop=True), scores_done)
                for buf in qk[p % 2]:
                    buf.free = [tok]
                scored[n] = (bk, tok)

            def maxima(n):
                p, u = divmod(n, NU)
                bk, tok = scored[n]
                DVE.wait(tok)
                for head, qt, at in SEGS[u]:
                    tok = DVE.do(lambda e, h=head, q=qt, at=at: e.tensor_reduce(
                        neg_max[:, p % 2, q, h:h + 1], bk.t[:, at:at + (q + 1) * P], AX.X, ALU.max, negate=True),
                        dve_max)
                scored[n] = (bk, tok)

            def exponentials(n):
                p, u = divmod(n, NU)
                bk, tok = scored.pop(n)
                par = p % 2
                pr = probs.take()
                ACTQ.wait(tok, *pr.free)
                if u == 0:
                    ACTQ.wait(*sums_free[par])
                for head, qt, at in SEGS[u]:
                    tok = ACTQ.do(lambda e, h=head, q=qt, at=at: e.activation(
                        pr.t[:, at:at + (q + 1) * P], bk.t[:, at:at + (q + 1) * P], ACT.Exp,
                        bias=neg_max[:, par, q, h:h + 1], accum_out=row_sum[:, par, q, h:h + 1]), act_exp)
                bk.free = [tok]
                probs_of[n] = (pr, tok)
                exp_of_pair[p] = tok

            def turn(n):
                u = n % NU
                pr, tok = probs_of.pop(n)
                cols = sum((qt + 1) * P for _, qt, _ in SEGS[u])
                bk = banks.take()
                PE.wait(tok, *bk.free)
                for k in range(cols // P):
                    tok = PE.do(lambda e, k=k: e.transpose(bk.t[:, k * P:(k + 1) * P], pr.t[:, k * P:(k + 1) * P],
                                                           ident[:, :]), turned if k == cols // P - 1 else None)
                pr.free = [tok]
                turned_of[n] = (bk, cols, tok)

            def split_turned(n):
                bk, cols, tok = turned_of[n]
                th, tl = pTh.take(), pTl.take()
                ACTQ.wait(*th.free)
                DVE.wait(*tl.free)
                bk.free = split_bank(bk.t[:, 0:cols], th.t[:, 0:cols], tl.t[:, 0:cols], [tok], P_SCALE)
                turned_of[n] = (th, tl, bk.free)

            def weigh(n):
                p, u = divmod(n, NU)
                th, tl, ready = turned_of.pop(n)
                o = o_banks[p % 2]
                PE.wait(*ready, *v_ready)
                if u == 0:
                    PE.wait(*o.free)
                for head, qt, at in SEGS[u]:
                    dst = o.t[:, (qt * 2 + head) * HEAD:(qt * 2 + head + 1) * HEAD]
                    dims = slice(p * P + head * HEAD, p * P + (head + 1) * HEAD)
                    for kt in range(qt + 1):
                        blk = slice(at + kt * P, at + (kt + 1) * P)
                        tok = three_pass(dst, th.t[:, blk], tl.t[:, blk], vh.t[:, kt, dims], vl.t[:, kt, dims],
                                         pv_done if kt == qt else None, first=kt == 0, last=kt == qt)
                th.free = tl.free = [tok]
                o_last[p] = tok

            def divide(p):
                par = p % 2
                o = o_banks[par]
                DVE.wait(exp_of_pair[p])
                tok = DVE.do(lambda e: e.tensor_scalar(scaled_sum[:, par], row_sum[:, par], pv_scale[:, 0:1], None,
                                                       ALU.mult), dve_small)
                sums_free[par] = [tok]
                DVE.wait(tok)
                tok = DVE.do(lambda e: e.reciprocal(inv_sum[:, par], scaled_sum[:, par]), dve_small)
                DVE.wait(tok, o_last[p], *attn.free)
                tok = DVE.do(lambda e: e.tensor_tensor(
                    attn.t[:, :, :].rearrange("p q (h d) -> p (q h) d", h=2),
                    o.t[:, :].rearrange("p (s d) -> p s d", d=HEAD),
                    inv_sum[:, par].rearrange("p q h -> p (q h)").unsqueeze(2).broadcast_to([P, NT * 2, HEAD]),
                    ALU.mult), dve_acc)
                o.free = attn.ready = [tok]

            def turn_heads(p):
                bk = banks.take()
                PE.wait(*attn.ready, *bk.free)
                for t in range(NT):
                    tok = PE.do(lambda e, t=t: e.transpose(bk.t[:, t * P:(t + 1) * P], attn.t[:, t, :], ident[:, :]),
                                turned if t == NT - 1 else None)
                attn.free = [tok]
                ACTQ.wait(*aTh.free)
                DVE.wait(*aTl.free)
                bk.free = split_bank(bk.t[:, :], aTh.t[:, :], aTl.t[:, :], [tok])
                aTh.ready = bk.free

            def project_out(p):
                PE.wait(*aTh.ready)
                if p == 0:
                    PE.wait(*sum_bank.free)
                tok = three_pass(sum_bank.t[:, :], woh[:, p, :], wol[:, p, :], aTh.t[:, :], aTl.t[:, :], y_done,
                                 first=p == 0, last=p == PAIRS - 1)
                aTh.free = aTl.free = [tok]
                return tok

            v_ready = []
            exp_of_pair = {}
            TURN_LAG, PV_LAG, HEADS_LAG, OUT_LAG, QK_AT = 2, 4, 5, 6, 2
            project_qk(0)
            for t in range(NT):
                for half in range(INNER // 512):
                    v_ready += project_v(t, half)
            LAST = NU * PAIRS
            for n in range(LAST + OUT_LAG + 1):
                if n % NU == QK_AT and n // NU + 1 < PAIRS:
                    project_qk(n // NU + 1)
                if n < LAST:
                    scores(n)
                if 0 <= n - TURN_LAG < LAST:
                    turn(n - TURN_LAG)
                if n < LAST:
                    maxima(n)
                if 0 <= n - TURN_LAG < LAST:
                    split_turned(n - TURN_LAG)
                if n < LAST:
                    exponentials(n)
                if 0 <= n - PV_LAG < LAST:
                    weigh(n - PV_LAG)
                    if (n - PV_LAG) % NU == NU - 1:
                        divide((n - PV_LAG) // NU)
                m = n - HEADS_LAG
                if m >= 0 and m % NU == NU - 1 and m < LAST:
                    turn_heads(m // NU)
                m = n - OUT_LAG
                if m >= 0 and m % NU == NU - 1 and m < LAST:
                    tok = project_out(m // NU)
                if n == LAST - 1:
                    xh.free = xl.free = [(qk_done, qk_done.value), (v_done, v_done.value)]
                yield n >= LAST - 1
            vh.free = vl.free = [(pv_done, pv_done.value)]
            yT = attn.t[:, :, :].rearrange("p t d -> p (t d)")
            ACTQ.wait(tok, *attn.free)
            tok = ACTQ.do(lambda e: e.activation(yT[:, :], sum_bank.t[:, :], ACT.Copy), act_copy)
            sum_bank.free = [tok]
            bk = banks.take()
            PE.wait(tok, *bk.free)
            for t in range(NT):
                tok = PE.do(lambda e, t=t: e.transpose(bk.t[:, t * P:(t + 1) * P], yT[:, t * P:(t + 1) * P],
                                                       ident[:, :]), turned if t == NT - 1 else None)
            attn.free = [tok]
            add_to_stream(b, bk, tok)

        sums_free = [[], []]

        ORDER = [("ff1", 0), ("ff1", 1), ("att", 0), ("ff1", 2), ("att", 1), ("ff2", 0), ("ff1", 3), ("att", 2),
                 ("ff2", 1), ("att", 3), ("ff2", 2), ("ff2", 3)]
        for b in range(B):
            if b > 0:
                x_tok.append(SP.do(lambda e, b=b: e.dma_start(xs[:, b * NT:(b + 1) * NT, :], chunk_of(x, b)),
                                   x_in[b], 16))
            xs_ready[b] = [x_tok[b]]
        def prologue(pos):
            kind, b = ORDER[pos]
            yield from layer_norm(b, normed[pos])
            if kind != "att" and pos > 0:
                yield
                yield from router(pos, b, *normed[pos])

        def layer(pos):
            kind, b = ORDER[pos]
            if kind == "att":
                yield from attention(b, *normed[pos], scale_tok[0])
            else:
                yield from feed_forward(pos, b, *normed[pos], prepare=pos == 0)
            if kind == "ff2":
                SP.wait(*xs_ready[b])
                SP.do(lambda e: e.dma_start(chunk_of(out, b), xs[:, b * NT:(b + 1) * NT, :]), stored, 16)

        scale_tok = []
        normed = [xnT.take() for _ in ORDER]
        for _ in prologue(0):
            pass
        ending = iter(())
        for pos in range(len(ORDER)):
            present = layer(pos)
            ahead = prologue(pos + 1) if pos + 1 < len(ORDER) else iter(())
            for steps, nearly_done in enumerate(present, 1):
                for _ in range(ENDING if steps == 1 else 99 if steps == 2 else 0):
                    next(ending, None)
                if pos == 0 and steps % 3 == 0 and steps // 3 <= len(wide_weights):
                    load_attention_weight(steps // 3 - 1)
                    if steps // 3 == len(wide_weights):
                        scale_tok.append(value_range())
                        vh.free = vl.free = raw_free[0] + raw_free[1]
                        for i in range(2):
                            probs.buffers[i].free = raw_w_free[i]
                if steps >= 10 and steps % 3 == 1:
                    next(ahead, None)
                if nearly_done:
                    break
            for _ in ahead:
                pass
            ending = present
        for _ in ending:
            pass
        last = (stored, stored.value)
        SP.wait(last, (route_stored, route_stored.value))

        block = ctx.enter_context(nc.Block())
        block.sync(SP.play)
        block.gpsimd(POOL.play)
        block.tensor(PE.play)
        block.scalar(ACTQ.play)
        block.vector(DVE.play)


_INS = ["L0_attn_inputs", "L0_attn_W_qkv", "L0_attn_W_out", "L0_ffn_Wg", "L0_ffn_routing_bias", "L0_ffn_W1",
        "L0_ffn_W2", "L0_ffn_W3", "L0_ffn_Ws1", "L0_ffn_Ws2", "L0_ffn_Ws3"]


def kernel(**inputs):
    import numpy as np
    import concourse.bacc as bacc
    from concourse.bass_utils import run_bass_kernel_spmd

    nc = bacc.Bacc("TRN2", target_bir_lowering=False, num_devices=1)
    arrays, args = {}, []
    for name in _INS:
        a = np.ascontiguousarray(inputs[name])
        arrays[f"in_{name}"] = a
        args.append(nc.dram_tensor(f"in_{name}", a.shape, mybir.dt.from_np(a.dtype), kind="ExternalInput").ap())
    shape = inputs["L0_attn_inputs"].shape
    out = nc.dram_tensor("out", shape, F32, kind="ExternalOutput").ap()
    experts = inputs["L0_ffn_Wg"].shape[0]
    tiles = shape[1] // P
    scratch = nc.dram_tensor("weight_scratch", (3 * shape[0], tiles * experts, P), F32, kind="Internal").ap()
    macaron(nc, *args, out, scratch)
    result = run_bass_kernel_spmd(nc, [arrays], core_ids=[0])
    return result.results[0]["out"]
```

```python
from contextlib import ExitStack

import concourse.bass as bass
from concourse import mybir

F32 = mybir.dt.float32
F32R = mybir.dt.float32r
F16 = mybir.dt.float16
BF16 = mybir.dt.bfloat16
U32 = mybir.dt.uint32
ALU = mybir.AluOpType
ACT = mybir.ActivationFunctionType
AX = mybir.AxisListType

P = 128
LN_EPS = 1e-5
TOP_K = 4
GLU_SCALE = 0.5 * 0.5
FF_SHARE = 0.55
SPLIT_LAG = 2
DOWN_LAG = 4
DVE_SHARE = 99
FIRST_SHARE = 2
LIGHT_SHARE = 1.0
WIDEN_AHEAD = 2
PREPARE_AHEAD = 3
MASKED = -8e30
P_SCALE = 4096.0


class Signal:

    def __init__(self, sem):
        self.sem, self.value = sem, 0


class Queue:

    def __init__(self):
        self.steps, self.passed = [], {}

    def wait(self, *tokens):
        for signal, value in tokens:
            if self.passed.get(signal, 0) < value:
                self.passed[signal] = value
                self.steps.append(lambda eng, s=signal.sem, v=value: eng.wait_ge(s, v))

    def do(self, issue, signal=None, by=1):
        if signal is None:
            self.steps.append(issue)
            return None
        self.steps.append(lambda eng: issue(eng).then_inc(signal.sem, by))
        signal.value += by
        return signal, signal.value

    def play(self, eng):
        for step in self.steps:
            step(eng)


class Buffer:

    def __init__(self, tensor):
        self.t, self.free, self.ready = tensor, [], []


class Ring:
    def __init__(self, buffers):
        self.buffers, self.taken = buffers, 0

    def take(self):
        self.taken += 1
        return self.buffers[(self.taken - 1) % len(self.buffers)]


def macaron(nc, x, w_qkv, w_out, w_gate, routing_bias, w1, w2, w3, ws1, ws2, ws3, out, weight_scratch):
    B, L, D = x.shape
    E, HID, _ = w1.shape
    NE = E + 1
    NT = L // P
    INNER = w_out.shape[0]
    HEAD = 64
    PAIRS = INNER // P
    RAW_TILES = [(j * P, min(P, HID - j * P)) for j in range((HID + P - 1) // P)]
    NJ = len(RAW_TILES)
    UNITS_ALL = NE * HID
    HT = (UNITS_ALL + P - 1) // P
    FIRST = [j * P for j in range(HT)]
    SIZE = [min(P, UNITS_ALL - u) for u in FIRST]
    OWNERS = [list(range(FIRST[j] // HID, (FIRST[j] + SIZE[j] - 1) // HID + 1)) for j in range(HT)]
    assert D == P and L == 512 and NJ == 3 and HID > P and 2 * HEAD == P

    with ExitStack() as ctx:
        def sb(name, shape, dt=F32):
            return ctx.enter_context(nc.sbuf_tensor(name, shape, dt))

        def bank(name):
            return Buffer(ctx.enter_context(nc.psum_tensor(name, [P, 512], F32)))

        def signal(name):
            return Signal(ctx.enter_context(nc.semaphore(name)))

        w1h, w1l = sb("w1h", [P, UNITS_ALL], F32R), sb("w1l", [P, UNITS_ALL], F32R)
        w2h, w2l = sb("w2h", [P, UNITS_ALL], F32R), sb("w2l", [P, UNITS_ALL], F32R)
        w3h, w3l = sb("w3h", [P, HT, D], F32R), sb("w3l", [P, HT, D], F32R)
        wqkvh, wqkvl = sb("wqkvh", [P, 3 * INNER], F32R), sb("wqkvl", [P, 3 * INNER], F32R)
        woh, wol = sb("woh", [P, PAIRS, D], F32R), sb("wol", [P, PAIRS, D], F32R)
        wgh, wgl = sb("wgh", [P, E], F32R), sb("wgl", [P, E], F32R)

        ident = sb("ident", [P, P])
        ident_b = sb("ident_b", [P, P], BF16)
        causal = sb("causal", [P, P], BF16)
        earlier = sb("earlier", [P, E, E])
        neg_half = sb("neg_half", [P, NT])
        bias_b = sb("bias_b", [P, E])
        v_max = sb("v_max", [P, 1])
        v_top = sb("v_top", [P, 1])
        v_pow = sb("v_pow", [P, 1])
        v_inv = sb("v_inv", [P, 1])
        v_scale = sb("v_scale", [P, 1])
        pv_scale = sb("pv_scale", [P, 1])

        xs = sb("xs", [P, B * NT, D])
        xs_ready = [[] for _ in range(B)]
        xn = Buffer(sb("xn", [P, NT, D]))
        stats = sb("stats", [P, NT, 6])
        moments = sb("moments", [P, NT, 2])
        var_eps = sb("var_eps", [P, NT])
        rstd = sb("rstd", [P, NT])
        xnT = Ring([(Buffer(sb(f"xnTh{i}", [P, L], F32R)), Buffer(sb(f"xnTl{i}", [P, L], F32R))) for i in range(3)])

        gate = sb("gate", [P, NT, E])
        top = sb("top", [P, NT])
        beats, ties = [xn.t[:, :, :].rearrange("p t d -> p (t d)")[:, k * NT * E * E:(k + 1) * NT * E * E]
                       .rearrange("p (t i j) -> p t i j", t=NT, i=E) for k in range(2)]
        rank = sb("rank", [P, NT, E])
        shifted = sb("shifted", [P, NT, E])
        expo = sb("expo", [P, NT, E])
        chosen = sb("chosen", [P, NT, E])
        total = sb("total", [P, NT])
        inv_total = sb("inv_total", [P, NT])
        route = Buffer(sb("route", [P, NT, NE]))
        routeT = xn.t[0:NT * NE, 2, :]
        wide = Ring([Buffer(sb(f"wide{i}", [P, NT, P])) for i in range(3)])

        glu = Ring([Buffer(sb(f"glu{i}", [P, L])) for i in range(4)])
        gluh = Ring([Buffer(sb(f"gluh{i}", [P, L], F32R)) for i in range(3)])
        glul = Ring([Buffer(sb(f"glul{i}", [P, L], F32R)) for i in range(3)])

        qk = [[Buffer(sb(f"{n}{i}", [P, L], F32R)) for n in ("qh", "ql", "kh", "kl")] for i in range(2)]
        vh, vl = Buffer(sb("vh", [P, NT, INNER], F16)), Buffer(sb("vl", [P, NT, INNER], F16))
        probs = Ring([Buffer(sb(f"probs{i}", [P, 512])) for i in range(3)])
        pTh = Ring([Buffer(sb(f"pTh{i}", [P, 512], F16)) for i in range(3)])
        pTl = Ring([Buffer(sb(f"pTl{i}", [P, 512], F16)) for i in range(3)])
        neg_max = sb("neg_max", [P, 2, NT, 2])
        row_sum = sb("row_sum", [P, 2, NT, 2])
        scaled_sum = sb("scaled_sum", [P, 2, NT, 2])
        inv_sum = sb("inv_sum", [P, 2, NT, 2])
        attn = Buffer(sb("attn", [P, NT, P]))
        aTh, aTl = Buffer(sb("aTh", [P, L], F32R)), Buffer(sb("aTl", [P, L], F32R))
        raw12 = [vh.t[:, :, :].rearrange("p t n -> p (t n)")[:, i * 1536:(i + 1) * 1536].bitcast(F32)
                 .rearrange("p (w j d) -> p w j d", w=2, j=3) for i in range(2)]
        raw3 = [vl.t[:, :, :].rearrange("p t n -> p (t n)")[:, i * 1024:(i + 1) * 1024].bitcast(F32)
                for i in range(2)]
        raw_w = [probs.buffers[i].t[:, :] for i in range(2)]

        banks = Ring([bank(f"bank{i}") for i in range(5)])
        down_bank = bank("down_bank")
        y_bank = bank("y_bank")
        o_bank = bank("o_bank")

        x_in = [signal(f"x_in{b}") for b in range(B)]
        small_in = signal("small_in")
        raw_in = [signal(f"raw_in{i}") for i in range(2)]
        raw_w_in = [signal(f"raw_w_in{i}") for i in range(2)]
        route_stored = signal("route_stored")
        wide_in = [signal(f"wide_in{i}") for i in range(3)]
        stored = signal("stored")
        consts_made = signal("consts_made")
        pool_split = signal("pool_split")
        pool_small = signal("pool_small")
        pool_weigh = signal("pool_weigh")
        turned = signal("turned")
        hidden_done = signal("hidden_done")
        down_done = signal("down_done")
        gate_done = signal("gate_done")
        qk_done = signal("qk_done")
        v_done = signal("v_done")
        scores_done = signal("scores_done")
        pv_done = signal("pv_done")
        y_done = signal("y_done")
        act_high = signal("act_high")
        act_tanh = signal("act_tanh")
        act_exp = signal("act_exp")
        act_copy = signal("act_copy")
        dve_low = signal("dve_low")
        dve_glu = signal("dve_glu")
        dve_acc = signal("dve_acc")
        dve_small = signal("dve_small")
        dve_max = signal("dve_max")

        SP, POOL, PE, ACTQ, DVE = Queue(), Queue(), Queue(), Queue(), Queue()

        def f32(ap):
            return ap.bitcast(F32)

        chunk_of = lambda t, b: t[b].rearrange("(t p) d -> p t d", p=P)
        x_tok = [SP.do(lambda e, b=b: e.dma_start(xs[:, b * NT:(b + 1) * NT, :], chunk_of(x, b)), x_in[b], 16)
                 for b in range(1)]
        wg_raw = attn.t[0:E, 0, :]
        SP.do(lambda e: e.dma_start(wg_raw, w_gate), small_in, 16)
        small_tok = SP.do(lambda e: e.dma_start(bias_b[:, :], routing_bias.rearrange("(a n) -> a n", a=1)
                                                .broadcast_to([P, E])), small_in, 16)

        raw_free = [[], []]
        raw_ready = {}

        def load_expert(n):
            i = n % 2
            SP.wait(*raw_free[i])
            srcs = [ws1, ws2] if n == 0 else [w1[n - 1], w2[n - 1]]
            for k, src in enumerate(srcs):
                SP.do(lambda e, k=k, src=src: e.dma_start(
                    raw12[i][:, k, 0:2, :], src[0:2 * P, :].rearrange("(j p) d -> p j d", p=P)), raw_in[i], 16)
                SP.do(lambda e, k=k, src=src: e.dma_start(raw12[i][0:HID - 2 * P, k, 2, :], src[2 * P:HID, :]),
                      raw_in[i], 16)
            left = n * HID % P
            if left:
                src = ws3 if n == 1 else w3[n - 2]
                SP.do(lambda e: e.dma_start(raw3[i][:, 0:left], src[:, HID - left:HID]), raw_in[i], 16)
            raw_ready[n] = SP.do(lambda e: e.dma_start(raw3[i][:, left:left + HID], ws3 if n == 0 else w3[n - 1]),
                                 raw_in[i], 16)

        raw_w_free = [[], []]
        wide_weights = [(w_qkv[:, c * 512:(c + 1) * 512], wqkvh[:, c * 512:(c + 1) * 512],
                         wqkvl[:, c * 512:(c + 1) * 512]) for c in range(3 * INNER // 512)]
        wide_weights += [(w_out.rearrange("(k p) d -> p k d", p=P)[:, 4 * c:4 * c + 4, :],
                          woh[:, 4 * c:4 * c + 4, :], wol[:, 4 * c:4 * c + 4, :]) for c in range(PAIRS // 4)]
        attn_weights = []

        def load_attention_weight(c):
            src, high, low = wide_weights[c]
            i = c % 2
            raw = raw_w[i] if c < 3 * INNER // 512 else raw_w[i].rearrange("p (k d) -> p k d", k=4)
            SP.wait(*raw_w_free[i])
            tok = SP.do(lambda e: e.dma_start(raw, src), raw_w_in[i], 16)
            ACTQ.wait(tok)
            tok = ACTQ.do(lambda e: e.activation(high, raw, ACT.Copy), act_high)
            POOL.wait(tok)
            tok = POOL.do(lambda e: e.tensor_tensor(low, raw, f32(high), ALU.subtract), pool_split)
            raw_w_free[i] = [tok]
            attn_weights.append(tok)

        POOL.do(lambda e: e.memset(ident[:, :], 0.0), consts_made)
        POOL.do(lambda e: e.memset(causal[:, :], 0.0), consts_made)
        POOL.do(lambda e: e.memset(earlier[:, :, :], 1.0), consts_made)
        POOL.do(lambda e: e.memset(route.t[:, :, 0], 1.0), consts_made)
        tok = POOL.do(lambda e: e.memset(neg_half[:, :], -0.5), consts_made)
        POOL.wait(tok)
        tok = POOL.do(lambda e: e.affine_select(out=ident[:, :], in_=ident[:, :], compare_op=ALU.not_equal, fill=1.0,
                                                base=0, pattern=[[-1, P]], channel_multiplier=1), consts_made)
        POOL.do(lambda e: e.affine_select(out=causal[:, :], in_=causal[:, :], compare_op=ALU.is_ge, fill=MASKED,
                                          base=0, pattern=[[-1, P]], channel_multiplier=1), consts_made)
        POOL.do(lambda e: e.affine_select(out=earlier[:, :, :], in_=earlier[:, :, :], compare_op=ALU.is_gt, fill=0.0,
                                          base=0, pattern=[[1, E], [-1, E]], channel_multiplier=0), consts_made)
        POOL.wait(tok)
        consts = POOL.do(lambda e: e.tensor_copy(ident_b[:, :], ident[:, :]), consts_made)

        bk = banks.take()
        PE.wait(consts, small_tok)
        tok = PE.do(lambda e: e.transpose(bk.t[:, 0:E], wg_raw, ident[0:E, 0:E]), turned)
        attn.free = [tok]
        ACTQ.wait(tok)
        tok = ACTQ.do(lambda e: e.activation(wgh[:, :], bk.t[:, 0:E], ACT.Copy), act_high)
        DVE.wait(tok)
        gate_weights = DVE.do(lambda e: e.tensor_tensor(wgl[:, :], bk.t[:, 0:E], f32(wgh[:, :]), ALU.subtract), dve_low)
        bk.free = [gate_weights]

        def split_bank(src, high, low, after, scale=None):
            ACTQ.wait(*after)
            t_high = ACTQ.do(lambda e: e.activation(high, src, ACT.Copy, scale=1.0 if scale is None else scale),
                             act_high)
            DVE.wait(t_high)
            hv = f32(high) if high.dtype == F32R else high
            if scale is None:
                t_low = DVE.do(lambda e: e.tensor_tensor(low, src, hv, ALU.subtract), dve_low)
            else:
                t_low = DVE.do(lambda e: e.scalar_tensor_tensor(low, src, scale, hv, ALU.mult, ALU.subtract), dve_low)
            return [t_high, t_low]

        expert_ready = {}

        def prepare_expert(n):
            i = n % 2
            PE.wait(raw_ready[n])
            ready = []
            for k, (high, low) in enumerate(((w1h, w1l), (w2h, w2l))):
                bk = banks.take()
                PE.wait(*bk.free)
                for j, (h0, m) in enumerate(RAW_TILES):
                    last = j == NJ - 1
                    tok = PE.do(lambda e, j=j, h0=h0, m=m, k=k, bk=bk: e.transpose(
                        bk.t[:, h0:h0 + m], raw12[i][0:m, k, j, :], ident[0:m, 0:m]), turned if last else None)
                bk.free = split_bank(bk.t[:, 0:HID], high[:, n * HID:(n + 1) * HID], low[:, n * HID:(n + 1) * HID], [tok])
                ready += bk.free
            bk = banks.take()
            PE.wait(*bk.free)
            tiles = [j for j in range(HT) if OWNERS[j][-1] == n]
            for k, j in enumerate(tiles):
                tok = PE.do(lambda e, k=k, j=j, bk=bk: e.transpose(
                    bk.t[0:SIZE[j], k * D:(k + 1) * D], raw3[i][:, k * P:k * P + SIZE[j]], ident[:, :]),
                    turned if j == tiles[-1] else None)
            raw_free[i] = [tok]
            full = [j for j in tiles if SIZE[j] == P]
            f = len(full)
            bk.free = split_bank(bk.t[:, 0:f * D], w3h[:, full[0]:full[0] + f, :].rearrange("p j d -> p (j d)"),
                                 w3l[:, full[0]:full[0] + f, :].rearrange("p j d -> p (j d)"), [tok])
            ready += bk.free
            for j in tiles[f:]:
                m = SIZE[j]
                bk.free = split_bank(bk.t[0:m, f * D:(f + 1) * D], w3h[0:m, j, :], w3l[0:m, j, :], [ready[-1]])
                ready += bk.free
            expert_ready[n] = ready

        def three_pass(ps, high, low, mhigh, mlow, signal=None, first=True, last=True):
            PE.do(lambda e: e.matmul(ps, high, mhigh, start=first, stop=False))
            PE.do(lambda e: e.matmul(ps, high, mlow, start=False, stop=False))
            return PE.do(lambda e: e.matmul(ps, low, mhigh, start=False, stop=last), signal)

        def layer_norm(b, halves):
            rows = [xs[:, b * NT + t, :] for t in range(NT)]
            DVE.wait(*xs_ready[b])
            for t in range(NT):
                tok = DVE.do(lambda e, t=t: e.bn_stats(stats[:, t, :], rows[t]), dve_small)
            DVE.wait(tok)
            for t in range(NT):
                tok = DVE.do(lambda e, t=t: e.bn_aggr(moments[:, t, :], stats[:, t, :]), dve_small)
            DVE.wait(tok)
            tok = DVE.do(lambda e: e.tensor_scalar(var_eps[:, :], moments[:, :, 1], LN_EPS, None, ALU.add), dve_small)
            POOL.wait(tok, consts)
            tok = POOL.do(lambda e: e.tensor_tensor(rstd[:, :], var_eps[:, :], neg_half[:, :], ALU.pow), pool_small)
            DVE.wait(tok, *xn.free)
            for t in range(NT):
                tok = DVE.do(lambda e, t=t: e.tensor_scalar(xn.t[:, t, :], rows[t], moments[:, t, 0:1],
                                                            rstd[:, t:t + 1], ALU.subtract, ALU.mult), dve_small)
            yield
            bk = banks.take()
            PE.wait(tok, *bk.free)
            for t in range(NT):
                tok = PE.do(lambda e, t=t: e.transpose(bk.t[:, t * P:(t + 1) * P], xn.t[:, t, :], ident[:, :]),
                            turned if t == NT - 1 else None)
            xn.free = [tok]
            xh, xl = halves
            ACTQ.wait(*xh.free)
            DVE.wait(*xl.free)
            bk.free = split_bank(bk.t[:, :], xh.t[:, :], xl.t[:, :], [tok])
            xh.ready = xl.ready = bk.free

        scratch_ready = {}

        def router(c, b, xh, xl):
            bk = banks.take()
            PE.wait(*bk.free, *xh.ready, gate_weights)
            for t in range(NT):
                s = slice(t * P, (t + 1) * P)
                tok = three_pass(bk.t[:, t * E:(t + 1) * E], xh.t[:, s], xl.t[:, s], wgh[:, :], wgl[:, :],
                                 gate_done if t == NT - 1 else None)
            rows_i = lambda a: a[:, :, :].unsqueeze(3).broadcast_to([P, NT, E, E])
            rows_j = lambda a: a[:, :, :].unsqueeze(2).broadcast_to([P, NT, E, E])
            over = lambda a: a[:, :].unsqueeze(2).broadcast_to([P, NT, E])

            def small(issue, *waits):
                DVE.wait(*waits)
                return DVE.do(issue, dve_small)

            tok = small(lambda e: e.tensor_tensor(gate[:, :, :], bk.t[:, 0:NT * E].rearrange("p (t n) -> p t n", t=NT),
                                                  bias_b[:, :].unsqueeze(1).broadcast_to([P, NT, E]), ALU.add),
                        tok, small_tok)
            bk.free = [tok]
            t_top = small(lambda e: e.tensor_reduce(top[:, :], gate[:, :, :], AX.X, ALU.max), tok)
            small(lambda e: e.tensor_tensor(beats, rows_j(gate), rows_i(gate), ALU.is_gt),
                  tok, *xn.free)
            tok = small(lambda e: e.tensor_tensor(ties, rows_j(gate), rows_i(gate), ALU.is_equal))
            t_shift = small(lambda e: e.tensor_tensor(shifted[:, :, :], gate[:, :, :], over(top), ALU.subtract), t_top)
            tok = small(lambda e: e.tensor_tensor(ties, ties,
                                                  earlier[:, :, :].unsqueeze(1).broadcast_to([P, NT, E, E]), ALU.mult),
                        tok, consts)
            ACTQ.wait(t_shift)
            t_exp = ACTQ.do(lambda e: e.activation(expo[:, :, :], shifted[:, :, :], ACT.Exp), act_exp)
            tok = small(lambda e: e.tensor_tensor(beats, beats, ties, ALU.add), tok)
            tok = small(lambda e: e.tensor_reduce(rank[:, :, :], beats, AX.X, ALU.add), tok)
            tok = small(lambda e: e.scalar_tensor_tensor(chosen[:, :, :], rank[:, :, :], float(TOP_K), expo[:, :, :],
                                                         ALU.is_lt, ALU.mult), tok, t_exp)
            tok = small(lambda e: e.tensor_reduce(total[:, :], chosen[:, :, :], AX.X, ALU.add), tok)
            tok = small(lambda e: e.reciprocal(inv_total[:, :], total[:, :]), tok)
            tok = small(lambda e: e.tensor_tensor(route.t[:, :, 1:NE], chosen[:, :, :], over(inv_total), ALU.mult),
                        tok, *route.free)
            yield
            bt = banks.take()
            PE.wait(tok, *bt.free)
            tok = PE.do(lambda e: e.transpose(bt.t[0:NT * NE, 0:P], route.t[:, :, :].rearrange("p t n -> p (t n)"),
                                              ident[:, :]), turned)
            route.free = [tok]
            DVE.wait(tok)
            tok = DVE.do(lambda e: e.tensor_copy(routeT, bt.t[0:NT * NE, 0:P]), dve_small)
            bt.free = [tok]
            SP.wait(tok)
            tok = SP.do(lambda e: e.dma_start(weight_scratch[c], routeT), route_stored, 16)
            xn.free = [tok]
            scratch_ready[c] = tok

        def widen(c, owners, j):
            n = wide.taken % 3
            buf = wide.take()
            SP.wait(scratch_ready[c], *buf.free)
            rows = weight_scratch[c].rearrange("(t n) p -> n t p", t=NT)
            for owner in owners:
                u0 = max(owner * HID - FIRST[j], 0) if len(owners) > 1 else 0
                u1 = min((owner + 1) * HID - FIRST[j], P) if len(owners) > 1 else P
                src = rows[owner:owner + 1].broadcast_to([u1 - u0, NT, P])
                tok = SP.do(lambda e, u0=u0, u1=u1, src=src: e.dma_start(buf.t[u0:u1, :, :], src), wide_in[n], 16)
            buf.ready = [tok]
            return buf

        def feed_forward(c, b, xh, xl, prepare):
            tiles = {}
            prepared = 0
            if prepare:
                load_expert(0)
                load_expert(1)
                prepare_expert(0)
                load_expert(2)
                prepared = 1
                for _ in router(c, b, xh, xl):
                    pass

            groups = []
            for j in range(HT):
                if OWNERS[j] != [0] and (not groups or OWNERS[j] != OWNERS[groups[-1][0]]):
                    groups.append([j])
                elif groups:
                    groups[-1].append(j)
            wides = {}

            def widen_group(g):
                if g < len(groups):
                    buf = widen(c, OWNERS[groups[g][0]], groups[g][0])
                    for j in groups[g]:
                        wides[j] = buf

            def hidden(j):
                m, cols = SIZE[j], slice(FIRST[j], FIRST[j] + SIZE[j])
                b1, b2 = banks.take(), banks.take()
                PE.wait(*b1.free, *xh.ready)
                for owner in OWNERS[j]:
                    PE.wait(*expert_ready[owner])
                t1 = three_pass(b1.t[0:m, :], w1h[:, cols], w1l[:, cols], xh.t[:, :], xl.t[:, :], hidden_done)
                PE.wait(*b2.free)
                t2 = three_pass(b2.t[0:m, :], w2h[:, cols], w2l[:, cols], xh.t[:, :], xl.t[:, :], hidden_done)
                g = glu.take()
                ACTQ.wait(t1, *g.free)
                tok = ACTQ.do(lambda e: e.activation(g.t[0:m, :], b1.t[0:m, :], ACT.Tanh, scale=0.5), act_tanh)
                DVE.wait(tok)
                tok = DVE.do(lambda e: e.scalar_tensor_tensor(g.t[0:m, :], g.t[0:m, :], 1.0, b1.t[0:m, :], ALU.add,
                                                              ALU.mult), dve_glu)
                b1.free = [tok]
                DVE.wait(t2, tok)
                tok = DVE.do(lambda e: e.tensor_tensor(g.t[0:m, :], g.t[0:m, :], b2.t[0:m, :], ALU.mult), dve_glu)
                b2.free = [tok]
                tiles[j] = (g, tok)

            def weight_hidden(j):
                if j not in wides:
                    return
                m = SIZE[j]
                g, tg = tiles[j]
                w = wides.pop(j)
                POOL.wait(tg, *w.ready)
                tok = POOL.do(lambda e: e.tensor_tensor(g.t[0:m, :], g.t[0:m, :],
                                                        w.t[0:m, :, :].rearrange("p t n -> p (t n)"), ALU.mult),
                              pool_weigh)
                w.free = [tok]
                tiles[j] = (g, tok)

            def split_hidden(j):
                m = SIZE[j]
                g, tg = tiles[j]
                gh, gl = gluh.take(), glul.take()
                ACTQ.wait(tg, *gh.free)
                th = ACTQ.do(lambda e: e.activation(gh.t[0:m, :], g.t[0:m, :], ACT.Copy), act_high)
                eng, done_by = (DVE, dve_low) if j % (FIRST_SHARE if c == 0 else DVE_SHARE) == 0 else (POOL, pool_split)
                eng.wait(th, tg, *gl.free)
                tl = eng.do(lambda e: e.tensor_tensor(gl.t[0:m, :], g.t[0:m, :], f32(gh.t[0:m, :]), ALU.subtract),
                            done_by)
                g.free = [th, tl]
                tiles[j] = (gh, gl, [th, tl])

            def down(j):
                m = SIZE[j]
                gh, gl, ready = tiles.pop(j)
                PE.wait(*ready)
                if j == 0:
                    PE.wait(*down_bank.free)
                tok = three_pass(down_bank.t[:, :], w3h[0:m, j, :], w3l[0:m, j, :], gh.t[0:m, :], gl.t[0:m, :],
                                 down_done, first=j == 0, last=j == HT - 1)
                gh.free = gl.free = [tok]
                return tok

            g_next = 0
            for i in range(HT + DOWN_LAG):
                if prepare and i < HT:
                    while prepared < NE and OWNERS[min(i + PREPARE_AHEAD, HT - 1)][-1] >= prepared:
                        prepare_expert(prepared)
                        prepared += 1
                        if prepared + 1 < NE:
                            load_expert(prepared + 1)
                if i >= DOWN_LAG:
                    tok = down(i - DOWN_LAG)
                if i < HT:
                    hidden(i)
                if SPLIT_LAG <= i < HT + SPLIT_LAG:
                    split_hidden(i - SPLIT_LAG)
                while i < HT and g_next < len(groups) and groups[g_next][0] <= i + WIDEN_AHEAD:
                    widen_group(g_next)
                    g_next += 1
                if i < HT:
                    weight_hidden(i)
                yield i >= HT - 1
                if i == HT - 1:
                    xh.free = xl.free = [(hidden_done, hidden_done.value)]
            yield True
            y = glu.take()
            ACTQ.wait(tok, *y.free)
            tok = ACTQ.do(lambda e: e.activation(y.t[:, :], down_bank.t[:, :], ACT.Copy, scale=GLU_SCALE), act_copy)
            down_bank.free = [tok]
            bk = banks.take()
            PE.wait(tok, *bk.free)
            for t in range(NT):
                tok = PE.do(lambda e, t=t: e.transpose(bk.t[:, t * P:(t + 1) * P], y.t[:, t * P:(t + 1) * P],
                                                       ident[:, :]), turned if t == NT - 1 else None)
            y.free = [tok]
            add_to_stream(b, bk, tok)

        def add_to_stream(b, bk, tok):
            rows = xs[:, b * NT:(b + 1) * NT, :].rearrange("p t d -> p (t d)")
            DVE.wait(tok)
            tok = DVE.do(lambda e: e.tensor_tensor(rows, rows, bk.t[:, :], ALU.add), dve_acc)
            bk.free = [tok]
            xs_ready[b] = [tok]

        def value_range():
            DVE.wait(*attn_weights)
            tok = DVE.do(lambda e: e.tensor_reduce(v_max[:, :], f32(wqkvh[:, 2 * INNER:3 * INNER]), AX.X, ALU.max,
                                                   apply_absolute_value=True), dve_small)
            POOL.wait(tok)
            tok = POOL.do(lambda e: e.partition_all_reduce(v_top[:, :], v_max[:, :], P, bass.bass_isa.ReduceOp.max),
                          pool_small)
            DVE.wait(tok)
            tok = DVE.do(lambda e: e.tensor_scalar(v_max[:, :], v_top[:, :], 2.0 ** -100, 2.0 ** 100, ALU.max,
                                                   ALU.min), dve_small)
            DVE.wait(tok)
            tok = DVE.do(lambda e: e.tensor_scalar(v_pow[:, :].bitcast(U32), v_max[:, :].bitcast(U32), 0x7F800000,
                                                   None, ALU.bitwise_and), dve_small)
            DVE.wait(tok)
            tok = DVE.do(lambda e: e.reciprocal(v_inv[:, :], v_pow[:, :]), dve_small)
            DVE.wait(tok)
            DVE.do(lambda e: e.tensor_scalar(v_scale[:, :], v_inv[:, :], 8.0, None, ALU.mult), dve_small)
            return DVE.do(lambda e: e.tensor_scalar(pv_scale[:, :], v_inv[:, :], 8.0, P_SCALE, ALU.mult, ALU.mult),
                          dve_small)

        UNITS = [[(0, 3)], [(0, 2), (0, 0)], [(1, 3)], [(1, 2), (1, 0)], [(0, 1), (1, 1)]]
        SEGS = []
        for unit in UNITS:
            at, segs = 0, []
            for head, qt in unit:
                segs.append((head, qt, at))
                at += (qt + 1) * P
            SEGS.append(segs)
        NU = len(UNITS)

        def attention(b, xh, xl, scale_tok):
            qk_ready, scored, probs_of, turned_of, o_last = {}, {}, {}, {}, {}

            def project_v(t, half):
                cols = slice(half * 512, (half + 1) * 512)
                wide_cols = slice(2 * INNER + half * 512, 2 * INNER + (half + 1) * 512)
                s = slice(t * P, (t + 1) * P)
                bk = banks.take()
                PE.wait(*bk.free, *xh.ready, *attn_weights)
                tok = three_pass(bk.t[:, :], xh.t[:, s], xl.t[:, s], wqkvh[:, wide_cols], wqkvl[:, wide_cols], v_done)
                ACTQ.wait(scale_tok, *vh.free)
                DVE.wait(scale_tok, *vl.free)
                bk.free = split_bank(bk.t[:, :], vh.t[:, t, cols], vl.t[:, t, cols], [tok], v_scale[:, 0:1])
                return bk.free

            def project_qk(p):
                bufs = qk[p % 2]
                ready = []
                for k in range(2):
                    cols = slice(k * INNER + p * P, k * INNER + (p + 1) * P)
                    high, low = bufs[2 * k], bufs[2 * k + 1]
                    bk = banks.take()
                    PE.wait(*bk.free, *xh.ready, *attn_weights)
                    tok = three_pass(bk.t[:, :], wqkvh[:, cols], wqkvl[:, cols], xh.t[:, :], xl.t[:, :], qk_done)
                    ACTQ.wait(*high.free)
                    DVE.wait(*low.free)
                    bk.free = split_bank(bk.t[:, :], high.t[:, :], low.t[:, :], [tok],
                                         HEAD ** -0.5 if k == 0 else None)
                    ready += bk.free
                qk_ready[p] = ready

            def scores(n):
                p, u = divmod(n, NU)
                qh, ql, kh, kl = qk[p % 2]
                bk = banks.take()
                PE.wait(*bk.free, *qk_ready[p], consts)
                first_head, tok = SEGS[u][0][0], None
                for head, qt, at in SEGS[u]:
                    if head != first_head:
                        PE.wait(tok)
                    rows = slice(head * HEAD, (head + 1) * HEAD)
                    q, keys = slice(qt * P, (qt + 1) * P), slice(0, (qt + 1) * P)
                    three_pass(bk.t[:, at:at + (qt + 1) * P], qh.t[rows, q], ql.t[rows, q],
                               kh.t[rows, keys], kl.t[rows, keys], last=False)
                    tok = PE.do(lambda e, a=at + qt * P: e.matmul(bk.t[:, a:a + P], ident_b[:, :], causal[:, :],
                                                                  start=False, stop=True), scores_done)
                for buf in qk[p % 2]:
                    buf.free = [tok]
                scored[n] = (bk, tok)

            def maxima(n):
                p, u = divmod(n, NU)
                bk, tok = scored[n]
                DVE.wait(tok)
                for head, qt, at in SEGS[u]:
                    tok = DVE.do(lambda e, h=head, q=qt, at=at: e.tensor_reduce(
                        neg_max[:, p % 2, q, h:h + 1], bk.t[:, at:at + (q + 1) * P], AX.X, ALU.max, negate=True),
                        dve_max)
                scored[n] = (bk, tok)

            def exponentials(n):
                p, u = divmod(n, NU)
                bk, tok = scored.pop(n)
                par = p % 2
                pr = probs.take()
                ACTQ.wait(tok, *pr.free)
                if u == 0:
                    ACTQ.wait(*sums_free[par])
                for head, qt, at in SEGS[u]:
                    tok = ACTQ.do(lambda e, h=head, q=qt, at=at: e.activation(
                        pr.t[:, at:at + (q + 1) * P], bk.t[:, at:at + (q + 1) * P], ACT.Exp,
                        bias=neg_max[:, par, q, h:h + 1], accum_out=row_sum[:, par, q, h:h + 1]), act_exp)
                bk.free = [tok]
                probs_of[n] = (pr, tok)
                exp_of_pair[p] = tok

            def turn(n):
                u = n % NU
                pr, tok = probs_of.pop(n)
                cols = sum((qt + 1) * P for _, qt, _ in SEGS[u])
                bk = banks.take()
                PE.wait(tok, *bk.free)
                for k in range(cols // P):
                    tok = PE.do(lambda e, k=k: e.transpose(bk.t[:, k * P:(k + 1) * P], pr.t[:, k * P:(k + 1) * P],
                                                           ident[:, :]), turned if k == cols // P - 1 else None)
                pr.free = [tok]
                turned_of[n] = (bk, cols, tok)

            def split_turned(n):
                bk, cols, tok = turned_of[n]
                th, tl = pTh.take(), pTl.take()
                ACTQ.wait(*th.free)
                DVE.wait(*tl.free)
                bk.free = split_bank(bk.t[:, 0:cols], th.t[:, 0:cols], tl.t[:, 0:cols], [tok], P_SCALE)
                turned_of[n] = (th, tl, bk.free)

            def weigh(n):
                p, u = divmod(n, NU)
                th, tl, ready = turned_of.pop(n)
                o = o_bank
                PE.wait(*ready, *v_ready)
                if u == 0:
                    PE.wait(*o.free)
                for head, qt, at in SEGS[u]:
                    dst = o.t[:, (qt * 2 + head) * HEAD:(qt * 2 + head + 1) * HEAD]
                    dims = slice(p * P + head * HEAD, p * P + (head + 1) * HEAD)
                    for kt in range(qt + 1):
                        blk = slice(at + kt * P, at + (kt + 1) * P)
                        tok = three_pass(dst, th.t[:, blk], tl.t[:, blk], vh.t[:, kt, dims], vl.t[:, kt, dims],
                                         pv_done if kt == qt else None, first=kt == 0, last=kt == qt)
                th.free = tl.free = [tok]
                o_last[p] = tok

            def divide(p):
                o = o_bank
                DVE.wait(inverse[p], o_last[p], *attn.free)
                tok = DVE.do(lambda e: e.tensor_tensor(
                    attn.t[:, :, :].rearrange("p q (h d) -> p (q h) d", h=2),
                    o.t[:, :].rearrange("p (s d) -> p s d", d=HEAD),
                    inv_sum[:, p % 2].rearrange("p q h -> p (q h)").unsqueeze(2).broadcast_to([P, NT * 2, HEAD]),
                    ALU.mult), dve_acc)
                o.free = attn.ready = [tok]

            def invert_sums(p):
                par = p % 2
                DVE.wait(exp_of_pair[p])
                tok = DVE.do(lambda e: e.tensor_scalar(scaled_sum[:, par], row_sum[:, par], pv_scale[:, 0:1], None,
                                                       ALU.mult), dve_small)
                sums_free[par] = [tok]
                DVE.wait(tok)
                inverse[p] = DVE.do(lambda e: e.reciprocal(inv_sum[:, par], scaled_sum[:, par]), dve_small)

            def turn_heads(p):
                bk = banks.take()
                PE.wait(*attn.ready, *bk.free)
                for t in range(NT):
                    tok = PE.do(lambda e, t=t: e.transpose(bk.t[:, t * P:(t + 1) * P], attn.t[:, t, :], ident[:, :]),
                                turned if t == NT - 1 else None)
                attn.free = [tok]
                ACTQ.wait(*aTh.free)
                DVE.wait(*aTl.free)
                bk.free = split_bank(bk.t[:, :], aTh.t[:, :], aTl.t[:, :], [tok])
                aTh.ready = bk.free

            def project_out(p):
                PE.wait(*aTh.ready)
                if p == 0:
                    PE.wait(*y_bank.free)
                tok = three_pass(y_bank.t[:, :], woh[:, p, :], wol[:, p, :], aTh.t[:, :], aTl.t[:, :], y_done,
                                 first=p == 0, last=p == PAIRS - 1)
                aTh.free = aTl.free = [tok]
                return tok

            v_ready = []
            exp_of_pair, inverse = {}, {}
            TURN_LAG, PV_LAG, HEADS_LAG, OUT_LAG, QK_AT = 2, 4, 5, 6, 2
            project_qk(0)
            for t in range(NT):
                for half in range(INNER // 512):
                    v_ready += project_v(t, half)
                    yield LIGHT_SHARE
            LAST = NU * PAIRS
            for n in range(LAST + OUT_LAG + 1):
                if n % NU == QK_AT and n // NU + 1 < PAIRS:
                    project_qk(n // NU + 1)
                if 0 <= n - TURN_LAG < LAST:
                    turn(n - TURN_LAG)
                if n < LAST:
                    scores(n)
                    maxima(n)
                if 0 <= n - TURN_LAG < LAST:
                    split_turned(n - TURN_LAG)
                if n < LAST:
                    exponentials(n)
                if n % NU == 0 and 0 < n <= LAST:
                    invert_sums(n // NU - 1)
                if 0 <= n - PV_LAG < LAST:
                    weigh(n - PV_LAG)
                    if (n - PV_LAG) % NU == NU - 1:
                        divide((n - PV_LAG) // NU)
                m = n - HEADS_LAG
                if m >= 0 and m % NU == NU - 1 and m < LAST:
                    turn_heads(m // NU)
                m = n - OUT_LAG
                if m >= 0 and m % NU == NU - 1 and m < LAST:
                    tok = project_out(m // NU)
                if n == LAST - 1:
                    xh.free = xl.free = [(qk_done, qk_done.value), (v_done, v_done.value)]
                yield FF_SHARE if n < LAST else LIGHT_SHARE
            vh.free = vl.free = [(pv_done, pv_done.value)]
            yT = attn.t[:, :, :].rearrange("p t d -> p (t d)")
            ACTQ.wait(tok, *attn.free)
            tok = ACTQ.do(lambda e: e.activation(yT[:, :], y_bank.t[:, :], ACT.Copy), act_copy)
            y_bank.free = [tok]
            bk = banks.take()
            PE.wait(tok, *bk.free)
            for t in range(NT):
                tok = PE.do(lambda e, t=t: e.transpose(bk.t[:, t * P:(t + 1) * P], yT[:, t * P:(t + 1) * P],
                                                       ident[:, :]), turned if t == NT - 1 else None)
            attn.free = [tok]
            add_to_stream(b, bk, tok)

        sums_free = [[], []]

        FF_LAYERS = [("ff1", b) for b in range(B)] + [("ff2", b) for b in range(B)]
        finished, norming = set(), []

        def prologue(kind, b, c, halves):
            needs = {"ff1": None, "att": ("ff1", b), "ff2": ("att", b)}[kind]
            while norming or needs is not None and needs not in finished:
                yield "blocked"
            norming.append(kind)
            yield from layer_norm(b, halves)
            if kind != "att":
                if c > 0:
                    yield
                    yield from router(c, b, *halves)
            norming.clear()

        def feed_forward_stream():
            ending = iter(())
            halves = ff_halves.take()
            for _ in prologue(*FF_LAYERS[0], 0, halves):
                pass
            for c, (kind, b) in enumerate(FF_LAYERS):
                present = feed_forward(c, b, *halves, prepare=c == 0)
                halves = ff_halves.take()
                ahead = prologue(*FF_LAYERS[c + 1], c + 1, halves) if c + 1 < len(FF_LAYERS) else iter(())
                steps = 0
                while True:
                    steps += 1
                    for _ in range(1 if steps <= DOWN_LAG else 99):
                        next(ending, None)
                    if steps == DOWN_LAG + 1 and c > 0:
                        done(*FF_LAYERS[c - 1])
                    nearly_done = next(present)
                    if c == 0 and steps % 3 == 0 and steps // 3 <= len(wide_weights):
                        load_attention_weight(steps // 3 - 1)
                        if steps // 3 == len(wide_weights):
                            scale_tok.append(value_range())
                            vh.free = vl.free = raw_free[0] + raw_free[1]
                            for i in range(2):
                                probs.buffers[i].free = raw_w_free[i]
                    if steps >= 10 and steps % 3 == 1:
                        next(ahead, None)
                    yield
                    if nearly_done:
                        break
                for said in ahead:
                    if said == "blocked":
                        yield
                ending = present
            for _ in ending:
                pass
            done(*FF_LAYERS[-1])

        def done(kind, b):
            finished.add((kind, b))
            if kind == "ff2":
                SP.wait(*xs_ready[b])
                SP.do(lambda e: e.dma_start(chunk_of(out, b), xs[:, b * NT:(b + 1) * NT, :]), stored, 16)

        def attention_stream():
            for b in range(B):
                for said in prologue("att", b, None, att_halves):
                    yield 1.0
                yield from attention(b, *att_halves, scale_tok[0])
                finished.add(("att", b))

        for b in range(B):
            if b > 0:
                x_tok.append(SP.do(lambda e, b=b: e.dma_start(xs[:, b * NT:(b + 1) * NT, :], chunk_of(x, b)),
                                   x_in[b], 16))
            xs_ready[b] = [x_tok[b]]
        scale_tok = []
        ff_halves, att_halves = Ring(xnT.buffers[0:2]), xnT.buffers[2]
        feeds, attends = feed_forward_stream(), attention_stream()
        while ("ff1", 0) not in finished:
            next(feeds)
        owed, share = 0.0, 1.0
        while share is not None:
            owed += share
            if owed >= 1.0:
                owed -= 1.0
                next(feeds, None)
            share = next(attends, None)
        for _ in feeds:
            pass
        last = (stored, stored.value)
        SP.wait(last, (route_stored, route_stored.value))

        block = ctx.enter_context(nc.Block())
        block.sync(SP.play)
        block.gpsimd(POOL.play)
        block.tensor(PE.play)
        block.scalar(ACTQ.play)
        block.vector(DVE.play)


_INS = ["L0_attn_inputs", "L0_attn_W_qkv", "L0_attn_W_out", "L0_ffn_Wg", "L0_ffn_routing_bias", "L0_ffn_W1",
        "L0_ffn_W2", "L0_ffn_W3", "L0_ffn_Ws1", "L0_ffn_Ws2", "L0_ffn_Ws3"]


def kernel(**inputs):
    import numpy as np
    import concourse.bacc as bacc
    from concourse.bass_utils import run_bass_kernel_spmd

    nc = bacc.Bacc("TRN2", target_bir_lowering=False, num_devices=1)
    arrays, args = {}, []
    for name in _INS:
        a = np.ascontiguousarray(inputs[name])
        arrays[f"in_{name}"] = a
        args.append(nc.dram_tensor(f"in_{name}", a.shape, mybir.dt.from_np(a.dtype), kind="ExternalInput").ap())
    shape = inputs["L0_attn_inputs"].shape
    out = nc.dram_tensor("out", shape, F32, kind="ExternalOutput").ap()
    experts = inputs["L0_ffn_Wg"].shape[0]
    tiles = shape[1] // P
    scratch = nc.dram_tensor("weight_scratch", (3 * shape[0], tiles * (experts + 1), P), F32, kind="Internal").ap()
    macaron(nc, *args, out, scratch)
    result = run_bass_kernel_spmd(nc, [arrays], core_ids=[0])
    return result.results[0]["out"]
```
